# Optimizing a Trainium2 kernel written in Bass

```python
import numpy as np
import jax
import jax.numpy as jnp

def _softmax(x, axis=-1):
    return jax.nn.softmax(x, axis=axis)

def _gelu(x):
    return jax.nn.gelu(x, approximate=True)

def _silu(x):
    return jax.nn.silu(x)

def _sigmoid(x):
    return jax.nn.sigmoid(x)

def _layernorm(x, axis=-1, eps=1e-05):
    m = jnp.mean(x, axis=axis, keepdims=True)
    v = jnp.var(x, axis=axis, keepdims=True)
    return (x - m) / jnp.sqrt(v + eps)

def _scatter_add(tgt, idx, src, axis=0):
    return tgt.at[idx].add(src)

def _segment_sum(src, seg, n):
    return jax.ops.segment_sum(src, seg, n)
kernel_name = 'mk_seq_postln_d1_jaxref_r8_f10c4a'

def setup_inputs(seed: int=0):
    np.random.seed(seed)
    _w = jnp.asarray

    def _L0_attn_setup():
        import jax, jax.numpy as jnp
        import numpy as np
        Q_DIM = 512
        N_HEADS = 32
        HEAD_DIM = 128
        INNER = N_HEADS * HEAD_DIM
        EPS = 1e-06

        def rms_norm(x, w):
            xf = x.astype(jnp.float32)
            var = jnp.mean(xf * xf, axis=-1, keepdims=True)
            return (w.astype(jnp.float32) * xf * jax.lax.rsqrt(var + EPS)).astype(x.dtype)
        key = jax.random.key(seed)
        ks = jax.random.split(key, 12)
        s = 1.0 / np.sqrt(Q_DIM)
        return {'hidden_states': jax.random.normal(ks[0], (2, 256, Q_DIM), dtype=jnp.float32), 'Wq': jax.random.normal(ks[1], (Q_DIM, INNER), dtype=jnp.float32) * s, 'bq': jnp.zeros((INNER,), dtype=jnp.float32), 'Wk': jax.random.normal(ks[2], (Q_DIM, INNER), dtype=jnp.float32) * s, 'bk': jnp.zeros((INNER,), dtype=jnp.float32), 'Wv': jax.random.normal(ks[3], (Q_DIM, INNER), dtype=jnp.float32) * s, 'bv': jnp.zeros((INNER,), dtype=jnp.float32), 'Wo': jax.random.normal(ks[4], (INNER, Q_DIM), dtype=jnp.float32) * s, 'bo': jnp.zeros((Q_DIM,), dtype=jnp.float32), 'gq': jnp.ones((INNER,), dtype=jnp.float32), 'gk': jnp.ones((INNER,), dtype=jnp.float32)}
    _L0_attn_in = _L0_attn_setup()

    def _L0_ffn_setup():
        import jax, jax.numpy as jnp
        import numpy as np
        D_MODEL = 512
        D_HIDDEN = 1376
        RANK = 16
        BATCH, SEQ = (2, 256)

        def _matmul_lora(x, w, a, b, scale=1.0):
            out = jnp.einsum('bsd,hd->bsh', x, w)
            out = out + jnp.einsum('bsr,hr->bsh', jnp.einsum('bsd,rd->bsr', x, a), b) * scale
            return out
        key = jax.random.key(seed)
        ks = jax.random.split(key, 10)
        s = 0.02
        return {'x': jax.random.normal(ks[0], (BATCH, SEQ, D_MODEL), jnp.float32), 'gate_w': jax.random.normal(ks[1], (D_HIDDEN, D_MODEL), jnp.float32) * s, 'up_w': jax.random.normal(ks[2], (D_HIDDEN, D_MODEL), jnp.float32) * s, 'down_w': jax.random.normal(ks[3], (D_MODEL, D_HIDDEN), jnp.float32) * s, 'gate_a': jax.random.normal(ks[4], (RANK, D_MODEL), jnp.float32) * s, 'gate_b': jax.random.normal(ks[5], (D_HIDDEN, RANK), jnp.float32) * s, 'up_a': jax.random.normal(ks[6], (RANK, D_MODEL), jnp.float32) * s, 'up_b': jax.random.normal(ks[7], (D_HIDDEN, RANK), jnp.float32) * s, 'down_a': jax.random.normal(ks[8], (RANK, D_HIDDEN), jnp.float32) * s, 'down_b': jax.random.normal(ks[9], (D_MODEL, RANK), jnp.float32) * s}
    _L0_ffn_in = _L0_ffn_setup()
    _d = {'L0_attn_hidden_states': _L0_attn_in['hidden_states'], 'L0_attn_Wq': _L0_attn_in['Wq'], 'L0_attn_bq': _L0_attn_in['bq'], 'L0_attn_Wk': _L0_attn_in['Wk'], 'L0_attn_bk': _L0_attn_in['bk'], 'L0_attn_Wv': _L0_attn_in['Wv'], 'L0_attn_bv': _L0_attn_in['bv'], 'L0_attn_Wo': _L0_attn_in['Wo'], 'L0_attn_bo': _L0_attn_in['bo'], 'L0_attn_gq': _L0_attn_in['gq'], 'L0_attn_gk': _L0_attn_in['gk'], 'L0_ffn_gate_w': _L0_ffn_in['gate_w'], 'L0_ffn_up_w': _L0_ffn_in['up_w'], 'L0_ffn_down_w': _L0_ffn_in['down_w'], 'L0_ffn_gate_a': _L0_ffn_in['gate_a'], 'L0_ffn_gate_b': _L0_ffn_in['gate_b'], 'L0_ffn_up_a': _L0_ffn_in['up_a'], 'L0_ffn_up_b': _L0_ffn_in['up_b'], 'L0_ffn_down_a': _L0_ffn_in['down_a'], 'L0_ffn_down_b': _L0_ffn_in['down_b']}
    _x0 = _d['L0_attn_hidden_states']
    _d['L0_attn_hidden_states'] = jax.random.normal(jax.random.fold_in(jax.random.key(seed), 1), (2, 512, 512), dtype=_x0.dtype)
    del _x0
    return _d

def reference(L0_attn_hidden_states, L0_attn_Wq, L0_attn_bq, L0_attn_Wk, L0_attn_bk, L0_attn_Wv, L0_attn_bv, L0_attn_Wo, L0_attn_bo, L0_attn_gq, L0_attn_gk, L0_ffn_gate_w, L0_ffn_up_w, L0_ffn_down_w, L0_ffn_gate_a, L0_ffn_gate_b, L0_ffn_up_a, L0_ffn_up_b, L0_ffn_down_a, L0_ffn_down_b):

    def _L0_attn_ref(hidden_states, Wq, bq, Wk, bk, Wv, bv, Wo, bo, gq, gk):
        import jax, jax.numpy as jnp
        import numpy as np
        Q_DIM = 512
        N_HEADS = 32
        HEAD_DIM = 128
        INNER = N_HEADS * HEAD_DIM
        EPS = 1e-06

        def rms_norm(x, w):
            xf = x.astype(jnp.float32)
            var = jnp.mean(xf * xf, axis=-1, keepdims=True)
            return (w.astype(jnp.float32) * xf * jax.lax.rsqrt(var + EPS)).astype(x.dtype)
        B, S, _ = hidden_states.shape
        q = hidden_states @ Wq + bq
        k = hidden_states @ Wk + bk
        v = hidden_states @ Wv + bv
        q = rms_norm(q, gq)
        k = rms_norm(k, gk)
        q = q.reshape(B, S, N_HEADS, HEAD_DIM).transpose(0, 2, 1, 3)
        k = k.reshape(B, S, N_HEADS, HEAD_DIM).transpose(0, 2, 1, 3)
        v = v.reshape(B, S, N_HEADS, HEAD_DIM).transpose(0, 2, 1, 3)
        scale = 1.0 / np.sqrt(HEAD_DIM)
        attn = jnp.einsum('bhqd,bhkd->bhqk', q.astype(jnp.float32), k.astype(jnp.float32)) * scale
        attn = jax.nn.softmax(attn, axis=-1)
        out = jnp.einsum('bhqk,bhkd->bhqd', attn, v.astype(jnp.float32))
        out = out.transpose(0, 2, 1, 3).reshape(B, S, INNER).astype(hidden_states.dtype)
        return out @ Wo + bo

    def _L0_ffn_ref(x, gate_w, up_w, down_w, gate_a, gate_b, up_a, up_b, down_a, down_b):
        import jax, jax.numpy as jnp
        import numpy as np
        D_MODEL = 512
        D_HIDDEN = 1376
        RANK = 16
        BATCH, SEQ = (2, 256)

        def _matmul_lora(x, w, a, b, scale=1.0):
            out = jnp.einsum('bsd,hd->bsh', x, w)
            out = out + jnp.einsum('bsr,hr->bsh', jnp.einsum('bsd,rd->bsr', x, a), b) * scale
            return out
        gate = _matmul_lora(x, gate_w, gate_a, gate_b)
        up = _matmul_lora(x, up_w, up_a, up_b)
        hidden = jax.nn.silu(gate) * up
        out = _matmul_lora(hidden, down_w, down_a, down_b)
        return out
    x = L0_attn_hidden_states
    x = _layernorm(x + _L0_attn_ref(x, L0_attn_Wq, L0_attn_bq, L0_attn_Wk, L0_attn_bk, L0_attn_Wv, L0_attn_bv, L0_attn_Wo, L0_attn_bo, L0_attn_gq, L0_attn_gk), axis=-1)
    x = _layernorm(x + _L0_ffn_ref(x, L0_ffn_gate_w, L0_ffn_up_w, L0_ffn_down_w, L0_ffn_gate_a, L0_ffn_gate_b, L0_ffn_up_a, L0_ffn_up_b, L0_ffn_down_a, L0_ffn_down_b), axis=-1)
    return x

_drawn_inputs = setup_inputs


def setup_inputs(seed=0):
    import zlib

    import numpy as np

    out = dict(_drawn_inputs(seed))
    spreads = {'L0_attn_bq': (0.0, 0.325),
     'L0_attn_bk': (0.0, 0.8),
     'L0_attn_bv': (0.0, 0.1),
     'L0_attn_bo': (0.0, 0.1),
     'L0_attn_gq': (1.0, 0.2),
     'L0_attn_gk': (1.0, 0.2)}
    factors = {'L0_ffn_gate_a': 8.0,
     'L0_ffn_gate_b': 8.0,
     'L0_ffn_up_a': 5.847,
     'L0_ffn_up_b': 6.036,
     'L0_ffn_down_a': 6.185,
     'L0_ffn_down_b': 6.22}
    for name, (base, spread) in spreads.items():
        noise = np.random.default_rng([zlib.crc32(name.encode()), seed]).standard_normal(out[name].shape)
        drawn = base * np.exp(spread * noise) if base else spread * noise
        out[name] = jnp.asarray(drawn.astype(out[name].dtype))
    for name, factor in factors.items():
        out[name] = (out[name] * factor).astype(out[name].dtype)
    return out
```

```python
import concourse.bass as bass
from concourse import mybir
from contextlib import ExitStack

F32 = mybir.dt.float32
F32R = mybir.dt.float32r
ALU = mybir.AluOpType
ACT = mybir.ActivationFunctionType
AX = mybir.AxisListType

P = 128
NB, S, D = 2, 512, 512
HEADS, DH = 32, 128
INNER = HEADS * DH
FF, RANK = 1376, 16
KC = D // P
TC = S // P
PAIRS = HEADS // 2
W2 = 2 * DH
RMS_EPS, LN_EPS = 1e-6, 1e-5
FLOAT_MIN = -3.4028234e38
GROUPS = FF // W2
REST = FF - GROUPS * W2
FC = GROUPS * 2 + 1
FIRST = ((0, 0), (1, 0), (0, 1), (1, 1))
LK = 80


def layer_kernel(nc, xT, x, wq, wk, wv, wo, bq, bk, bv, bo, gq, gk,
                 gate_w, up_w, down_w, lora_a, lora_b, x1_dram, out):
    ctx = ExitStack()
    with ctx:
        def sem(name):
            return ctx.enter_context(nc.semaphore(name))

        O_BANK = (4, 7)
        bank = [ctx.enter_context(nc.psum_tensor(f"bank{i}", [P, 512], F32)) for i in range(8)]

        def const(name, shape):
            return ctx.enter_context(nc.sbuf_tensor(name, shape, F32))

        ident = const("ident", [P, P])
        bq_c = const("bq_c", [P, HEADS])
        bk_c = const("bk_c", [P, HEADS])
        bv_c = const("bv_c", [P, HEADS])
        gqk = const("gqk", [P, HEADS])
        gk_c = const("gk_c", [P, HEADS])
        bqg = const("bqg", [P, HEADS])
        rq = const("rq", [P, TC])
        neg_rq = const("neg_rq", [P, TC])
        row_max = const("row_max", [P, 8])
        neg_max = const("neg_max", [P, 8])
        carrier = const("carrier", [P, 8])
        row_sum = const("row_sum", [P, 8])
        inv_sum = const("inv_sum", [P, 8])
        ln_stats = const("ln_stats", [P, TC, 6])
        ln_mv = const("ln_mv", [P, TC, 2])
        ln_rstd = const("ln_rstd", [P, TC])

        with ExitStack() as region:
            def sa(name, shape, dt=F32):
                return region.enter_context(nc.sbuf_tensor(name, shape, dt))
            ks = sa("ks", [P, HEADS, S])
            qs = sa("qs", [P, HEADS, S])
            w_stage = [sa(f"w_stage{i}", [P, KC, W2]) for i in range(2)]
            slots = sa("slots", [P, 8, S])
            xT_hi = sa("xT_hi", [P, KC, S], F32R)
            xT_lo = sa("xT_lo", [P, KC, S], F32R)
            w_hi = [sa(f"w_hi{i}", [P, KC, W2], F32R) for i in range(2)]
            w_lo = [sa(f"w_lo{i}", [P, KC, W2], F32R) for i in range(2)]
            qk_hi = sa("qk_hi", [P, 2, S], F32R)
            qk_lo = sa("qk_lo", [P, 2, S], F32R)
            pT_hi = sa("pT_hi", [P, 2, S], F32R)
            pT_lo = sa("pT_lo", [P, 2, S], F32R)
            rk_rows = sa("rk_rows", [P, S])
            bo_rows = sa("bo_rows", [P, D])
        v_hi, v_lo = w_hi[1], w_lo[1]
        ones = bo_rows[:, 0:P]

        with ExitStack() as region:
            def sf(name, shape, dt=F32):
                return region.enter_context(nc.sbuf_tensor(name, shape, dt))
            x1_rows = sf("x1_rows", [P, 4, D])
            lb_f = sf("lb_f", [P, 3, W2])
            la = sf("la", [P, 3, D], F32R)
            lb = sf("lb", [P, 3, W2], F32R)
            gu_stage = [sf(f"gu_stage{i}", [P, KC, W2]) for i in range(2)]
            gu_hi = [[sf(f"gu_hi{j}{i}", [P, KC, P], F32R) for i in range(2)] for j in range(2)]
            gu_lo = [[sf(f"gu_lo{j}{i}", [P, KC, P], F32R) for i in range(2)] for j in range(2)]
            x1T_hi = [sf("x1T_hi0", [P, KC, S], F32R)]
            x1T_lo = [sf("x1T_lo0", [P, KC, S], F32R)]
            x1T_hi.append(sf("x1T_hi1", [P, KC, S], F32R))
            x1T_lo.append(sf("x1T_lo1", [P, KC, S], F32R))
            wd = sf("wd", [P, FC, D])
            wd_hi = sf("wd_hi", [P, 2, D], F32R)
            wd_lo = sf("wd_lo", [P, 2, D], F32R)
            hid_hi = sf("hid_hi", [P, FC, NB * S], F32R)
            hid_lo = sf("hid_lo", [P, FC, NB * S], F32R)
            act_f = sf("act_f", [P, 2, S])
        la_f = x1_rows[:, 0:3, :]

        def f(ap):
            return ap.bitcast(F32)

        const_in = sem("const_in")
        ident_zero = sem("ident_zero")
        ident_ready = sem("ident_ready")
        ones_ready = sem("ones_ready")
        bias_ready = sem("bias_ready")
        x_in = sem("x_in")
        xT_hi_ready = sem("xT_hi_ready")
        xT_ready = sem("xT_ready")
        w_in = [sem(f"w_in{i}") for i in range(2)]
        w_hi_ready = [sem(f"w_hi_ready{i}") for i in range(2)]
        w_ready = [sem(f"w_ready{i}") for i in range(2)]
        acc_zero = sem("acc_zero")
        proj_done = sem("proj_done")
        proj_free = sem("proj_free")
        sq_added = sem("sq_added")
        rms_sum = sem("rms_sum")
        rms_step = sem("rms_step")
        qk_hi_ready = sem("qk_hi_ready")
        qk_ready = sem("qk_ready")
        s_done = sem("s_done")
        s_free = sem("s_free")
        max_ready = sem("max_ready")
        exp_done = sem("exp_done")
        inv_ready = sem("inv_ready")
        p_ready = sem("p_ready")
        pT_done = sem("pT_done")
        pT_hi_ready = sem("pT_hi_ready")
        pT_ready = sem("pT_ready")
        pT_used = sem("pT_used")
        o_free = sem("o_free")
        v_done = sem("v_done")
        v_hi_ready = sem("v_hi_ready")
        v_ready = sem("v_ready")
        oT_hi_ready = sem("oT_hi_ready")
        oT_ready = sem("oT_ready")
        oT_used = sem("oT_used")
        res_in = sem("res_in")
        res_ready = sem("res_ready")
        merged = sem("merged")
        ln_sum = sem("ln_sum")
        ln_stat = sem("ln_stat")
        ln_mean = sem("ln_mean")
        ln_var = sem("ln_var")
        ln_sqrt = sem("ln_sqrt")
        ln_inv = sem("ln_inv")
        ln_done = sem("ln_done")
        x1_out = [sem(f"x1_out{i}") for i in range(NB)]
        la_in = sem("la_in")
        lora_zero = sem("lora_zero")
        la_ready = sem("la_ready")
        gu_in = sem("gu_in")
        lb_ready = sem("lb_ready")
        fold_done = sem("fold_done")
        w_eff = sem("w_eff")
        gu_hi_ready = sem("gu_hi_ready")
        gu_ready = sem("gu_ready")
        wd_in = sem("wd_in")
        x1_in = [sem(f"x1_in{i}") for i in range(4)]
        x1T_done = sem("x1T_done")
        x1T_hi_ready = sem("x1T_hi_ready")
        x1T_ready = sem("x1T_ready")
        gate_done = sem("gate_done")
        up_done = sem("up_done")
        silu_done = sem("silu_done")
        h_done = sem("h_done")
        h_hi_ready = sem("h_hi_ready")
        h_ready = sem("h_ready")
        wd_hi_ready = sem("wd_hi_ready")
        wd_ready = sem("wd_ready")
        wd_used = sem("wd_used")
        down_done = sem("down_done")
        out_done = [sem(f"out_done{i}") for i in range(4)]

        USES = (2 * PAIRS + PAIRS // 2, PAIRS + PAIRS // 2)

        def use0(b, phase):
            return b * USES[0] + {"project": 0, "attend": PAIRS, "merge": 2 * PAIRS}[phase]

        def use1(b, phase):
            return b * USES[1] + {"project": 0, "merge": PAIRS}[phase]

        def free_wd(eng, n):
            if n % FC == FC - 1:
                eng.wait_ge(down_done, TC * (n // FC + 1))
            else:
                eng.wait_ge(wd_used, (FC - 1) * (n // FC) + n % FC + 1)

        def roots_out(act, b):
            for c in range(TC):
                act.wait_ge(ln_var, TC * (NB + b) + c + 1)
                nc.scalar.activation(ln_rstd[:, c:c + 1], ln_rstd[:, c:c + 1], ACT.Sqrt).then_inc(ln_sqrt, 1)
                if c:
                    store_out(act, b, c - 1)
            store_out(act, b, TC - 1)

        def store_out(act, b, c):
            act.wait_ge(ln_done, TC * (NB + b) + c + 1)
            act.dma_start(out[(TC * b + c) * P:(TC * b + c + 1) * P, :], x1_rows[:, c, :]).then_inc(out_done[c], 16)

        def flat(t, part):
            half = KC * W2 // 2
            return t[:, :, :].rearrange("p k n -> p (k n)")[:, part * half:(part + 1) * half]

        block = ctx.enter_context(nc.Block())

        @block.sync
        def _(sp):
            wq_v, wk_v, wv_v, gate_v, up_v = (w.rearrange("(k p) n -> p k n", p=P)
                                              for w in (wq, wk, wv, gate_w, up_w))
            wo_v = wo.rearrange("(h p) n -> p h n", p=P)
            x1_v = x1_dram.rearrange("(c p) d -> p c d", p=P)

            def load_w(i, use, src):
                sp.wait_ge(w_ready[i], use)
                sp.dma_start(w_stage[i][:, :, :], src).then_inc(w_in[i], 16)

            def load_qk(b, p):
                load_w(0, use0(b, "project") + p, wq_v[:, :, bass.ds(p * W2, W2)])
                load_w(1, use1(b, "project") + p, wk_v[:, :, bass.ds(p * W2, W2)])

            def load_wo(b, p):
                for i, use in ((0, use0(b, "merge") + p), (1, use1(b, "merge") + p)):
                    sp.wait_ge(w_ready[i], use)
                    sp.dma_start(w_stage[i][:, :, :].rearrange("p k n -> p (k n)").rearrange("p (h n) -> p h n", h=2),
                                 wo_v[:, bass.ds(4 * p + 2 * i, 2), :]).then_inc(w_in[i], 16)

            def load_xT(b):
                sp.dma_start(slots[:, 4:8, :], xT[:, b * S:(b + 1) * S].rearrange("(k p) t -> p k t", p=P))\
                    .then_inc(x_in, 16)

            def load_gu(g, w):
                sp.dma_start(gu_stage[0][:, :, 0:w], gate_v[:, :, bass.ds(g * W2, w)]).then_inc(gu_in, 16)
                sp.dma_start(gu_stage[1][:, :, 0:w], up_v[:, :, bass.ds(g * W2, w)]).then_inc(gu_in, 16)
                for r in range(3):
                    sp.dma_start(lb_f[32 * r:32 * r + RANK, :, 0:w], lora_b[:, :, bass.ds(g * W2, w)])\
                        .then_inc(gu_in, 16)

            def load_x1(n):
                sp.dma_start(x1_rows[:, n % 4, :], x1_v[:, n, :]).then_inc(x1_in[n % 4], 16)

            load_xT(0)
            sp.dma_start(w_stage[0][:, :, :], wq_v[:, :, 0:W2]).then_inc(w_in[0], 16)
            sp.dma_start(w_stage[1][:, :, :], wk_v[:, :, 0:W2]).then_inc(w_in[1], 16)
            for dst, src in ((bq_c, bq), (bk_c, bk), (bv_c, bv), (gqk, gq), (gk_c, gk)):
                sp.dma_start(dst[:, :], src).then_inc(const_in, 16)
            for b in range(NB):
                if b:
                    load_qk(b, 0)
                with sp.Fori(1, PAIRS) as p:
                    load_qk(b, p)
                with sp.Fori(0, PAIRS) as p:
                    load_w(0, use0(b, "attend") + p, wv_v[:, :, bass.ds(p * W2, W2)])
                load_wo(b, 0)
                sp.wait_ge(pT_done, TC * HEADS * (b + 1))
                if b == 0:
                    load_xT(1)
                sp.dma_start(slots[:, 0:TC, :], x[b * S:(b + 1) * S, :].rearrange("(c p) d -> p c d", p=P))\
                    .then_inc(res_in, 16)
                sp.dma_start(bo_rows[:, :], bo.partition_broadcast(P)).then_inc(res_in, 16)
                if b == NB - 1:
                    sp.wait_ge(lora_zero, 2)
                    for r in range(3):
                        sp.dma_start(la_f[32 * r:32 * r + RANK, :, :], lora_a).then_inc(la_in, 16)
                    load_gu(0, W2)
                    sp.wait_ge(la_ready, 2)
                    sp.wait_ge(x1_out[0], 16 * TC)
                    for n in range(TC):
                        load_x1(n)
                with sp.Fori(1, PAIRS // 2) as p:
                    load_wo(b, p)

            sp.wait_ge(gu_ready, 4)
            sp.wait_ge(lb_ready, 2)
            load_gu(1, W2)
            sp.wait_ge(x1_out[1], 16 * TC)
            sp.wait_ge(x1T_done, TC)
            for n in range(TC, 2 * TC):
                load_x1(n)
            sp.dma_start(wd[:, 0:2 * GROUPS, :], down_w[0:GROUPS * W2, :].rearrange("(j p) n -> p j n", p=P))\
                .then_inc(wd_in, 16)
            sp.dma_start(wd[0:REST, 2 * GROUPS, :], down_w[GROUPS * W2:FF, :]).then_inc(wd_in, 16)
            with sp.Fori(2, GROUPS) as g:
                sp.wait_ge(gu_ready, 4 * g)
                load_gu(g, W2)
            sp.wait_ge(gu_ready, 4 * GROUPS)
            sp.wait_ge(lb_ready, 2 * GROUPS)
            load_gu(GROUPS, REST)
            sp.wait_ge(x1T_done, 2 * TC)
            for n in range(TC):
                load_x1(n)
            for n in range(TC, 2 * TC):
                sp.wait_ge(out_done[n % 4], 16)
                load_x1(n)
            for i in range(4):
                sp.wait_ge(out_done[i], 32)

        @block.gpsimd
        def _(pool):
            pool.sem_inc(sq_added, 2)
            pool.sem_inc(h_ready, 2)
            pool.memset(ident[:, :], 0.0).then_inc(ident_zero, 1)
            pool.memset(ones, 1.0).then_inc(ones_ready, 1)
            pool.wait_ge(ident_zero, 1)
            pool.affine_select(out=ident[:, :], in_=ident[:, :], compare_op=ALU.not_equal, fill=1.0,
                               base=0, pattern=[[-1, P]], channel_multiplier=1).then_inc(ident_ready, 1)
            for b in range(NB):
                h0 = HEADS * b
                pool.wait_ge(xT_ready, KC * (b + 1))
                pool.memset(slots[:, 4:6, :], 0.0).then_inc(acc_zero, 1)
                if b:
                    pool.memset(ones, 1.0).then_inc(ones_ready, 1)
                pool.wait_ge(acc_zero, b + 1)
                with pool.Fori(0, PAIRS) as p:
                    for u in range(4):
                        unit = 4 * (b * PAIRS + p) + u
                        pool.wait_ge(proj_free, unit + 5)
                        pool.wait_ge(sq_added, unit + 2)
                        acc = slots[:, 4 + u // 2, :]
                        nc.gpsimd.tensor_tensor(acc, acc, slots[:, 6 + u % 2, :], ALU.add).then_inc(sq_added, 1)

                def split_qk(h, hh):
                    for i in range(2):
                        pool.wait_ge(qk_hi_ready, 2 * h + 1 + i)
                        nc.gpsimd.tensor_tensor(qk_lo[:, 1 - i, :], (ks, qs)[i][:, hh, :], f(qk_hi[:, 1 - i, :]),
                                                ALU.subtract).then_inc(qk_ready, 1)

                def neg_maxima(h, e, c):
                    s = TC * e + c
                    pool.wait_ge(s_free, TC * h + c + 3)
                    nc.gpsimd.tensor_tensor(neg_max[:, s:s + 1], row_max[:, s:s + 1], neg_rq[:, c:c + 1],
                                            ALU.mult).then_inc(max_ready, 1)

                split_qk(h0, 0)
                pool.wait_ge(rms_step, 6 * b + 6)
                for c in range(TC):
                    neg_maxima(h0, 0, c)
                split_qk(h0 + 1, 1)
                with pool.Fori(0, PAIRS - 1) as p:
                    for e in range(2):
                        hh = 2 * p + e
                        for c in range(TC):
                            neg_maxima(h0 + hh + 1, 1 - e, c)
                            if e == 0 and c in (1, 2):
                                pool.wait_ge(w_hi_ready[0], 2 * (use0(b, "attend") + p + 1) + c)
                                op = nc.gpsimd.tensor_tensor(flat(w_lo[0], c - 1), flat(w_stage[0], c - 1),
                                                             f(flat(w_hi[0], c - 1)), ALU.subtract)
                                if c == 2:
                                    op.then_inc(w_ready[0], 1)
                        split_qk(h0 + hh + 2, hh + 2)
                for c in range(TC):
                    neg_maxima(h0 + HEADS - 1, 1, c)

                def oT_low(hh):
                    for e in range(2):
                        pool.wait_ge(oT_hi_ready, h0 + hh + e + 1)
                        nc.gpsimd.tensor_tensor(qk_lo[:, e, :], qs[:, hh + e, :], f(qk_hi[:, e, :]),
                                                ALU.subtract).then_inc(oT_ready, 1)
                if b == NB - 1:
                    pool.wait_ge(s_done, TC * HEADS * NB)
                    pool.memset(la_f, 0.0).then_inc(lora_zero, 1)
                    pool.memset(lb_f[:, :, :], 0.0).then_inc(lora_zero, 1)
                oT_low(0)
                oT_low(2)
                pool.wait_ge(res_in, 32 * (b + 1))
                for c in range(TC):
                    nc.gpsimd.tensor_tensor(slots[:, c, :], slots[:, c, :], bo_rows[:, :], ALU.add)\
                        .then_inc(res_ready, 1)
                with pool.Fori(2, PAIRS) as p:
                    oT_low(2 * p)
                for c in range(TC):
                    pool.wait_ge(ln_done, TC * b + c + 1)
                    pool.dma_start(x1_dram[(TC * b + c) * P:(TC * b + c + 1) * P, :], slots[:, c, :])\
                        .then_inc(x1_out[b], 16)

            def hid_low(n, par, j, b, rows):
                pool.wait_ge(h_hi_ready, n + 1)
                nc.gpsimd.tensor_tensor(hid_lo[0:rows, j, b * S:(b + 1) * S], act_f[0:rows, par, :],
                                        f(hid_hi[0:rows, j, b * S:(b + 1) * S]), ALU.subtract).then_inc(h_ready, 1)
            for n, (j, b) in enumerate(FIRST):
                hid_low(n, n % 2, j, b, P)
            with pool.Fori(1, GROUPS) as g:
                for jj in range(2):
                    for b in range(NB):
                        hid_low(4 * g + 2 * jj + b, b, 2 * g + jj, b, P)
            for b in range(NB):
                hid_low(4 * GROUPS + b, b, 2 * GROUPS, b, REST)

        @block.scalar
        def _(act):
            act.sem_inc(proj_free, 4)
            act.sem_inc(o_free, 2)

            def split_xT(b):
                act.wait_ge(x_in, 16 * (b + 1))
                for k in range(KC):
                    nc.scalar.activation(xT_hi[:, k, :], slots[:, 4 + k, :], ACT.Copy).then_inc(xT_hi_ready, 1)

            def x1T_high(n):
                act.wait_ge(x1T_done, n + 1)
                nc.scalar.activation(x1T_hi[n // TC][:, :, (n % TC) * P:(n % TC + 1) * P],
                                     bank[4 + n % 2][:, :].rearrange("p (k t) -> p k t", k=KC), ACT.Copy)\
                    .then_inc(x1T_hi_ready, 1)

            def gu_high(g, jj, w):
                act.wait_ge(w_eff, 6 * g + 4)
                for i in range(2):
                    nc.scalar.activation(gu_hi[jj][i][:, :, 0:w], gu_stage[i][:, :, jj * P:jj * P + w], ACT.Copy)\
                        .then_inc(gu_hi_ready, 1)

            split_xT(0)
            act.wait_ge(bias_ready, 2)
            for b in range(NB):
                h0 = HEADS * b
                act.wait_ge(xT_ready, KC * (b + 1))
                with act.Fori(0, PAIRS) as p:
                    for u in range(4):
                        unit = 4 * (b * PAIRS + p) + u
                        hh = 2 * p + u % 2
                        src = bank[4 + u][:, :]
                        act.wait_ge(sq_added, unit + 1)
                        act.wait_ge(proj_done, unit + 1)
                        if u < 2:
                            nc.scalar.activation(qs[:, hh, :], src, ACT.Identity, bias=bqg[:, bass.ds(hh, 1)],
                                                 scale=gqk[:, bass.ds(hh, 1)])
                        else:
                            nc.scalar.activation(ks[:, hh, :], src, ACT.Identity, bias=bk_c[:, bass.ds(hh, 1)])
                        nc.scalar.activation(slots[:, 6 + u % 2, :], src, ACT.Square,
                                             bias=(bq_c, bk_c)[u // 2][:, bass.ds(hh, 1)]).then_inc(proj_free, 1)

                def split_qk(hh):
                    for i in range(2):
                        nc.scalar.activation(qk_hi[:, 1 - i, :], (ks, qs)[i][:, hh, :], ACT.Copy)\
                            .then_inc(qk_hi_ready, 1)

                def exps(h, e, c):
                    s = TC * e + c
                    act.wait_ge(max_ready, TC * h + c + 1)
                    nc.scalar.activation(slots[:, s, :], slots[:, s, :], ACT.Exp, bias=neg_max[:, s:s + 1],
                                         scale=rq[:, c:c + 1], accum_out=row_sum[:, s:s + 1]).then_inc(exp_done, 1)

                def pT_high(h, j):
                    act.wait_ge(pT_done, TC * h + j + 1)
                    act.wait_ge(pT_used, TC * h + j + 1)
                    nc.scalar.activation(pT_hi[:, j % 2, :], bank[2 + j % 2][:, :], ACT.Copy).then_inc(pT_hi_ready, 1)

                def v_high(pair):
                    for half in range(2):
                        act.wait_ge(v_done, 2 * pair + half + 1)
                        if half == 0:
                            act.wait_ge(pT_used, TC * 2 * pair + 2)
                        nc.scalar.activation(v_hi[:, 2 * half:2 * half + 2, :],
                                             bank[5 + half][:, :].rearrange("p (c n) -> p c n", c=2),
                                             ACT.Copy).then_inc(v_hi_ready, 1)

                def store_o(h, e, hh):
                    act.wait_ge(pT_used, TC * h + TC + 2)
                    nc.scalar.activation(qs[:, hh, :], bank[O_BANK[e]][:, :], ACT.Identity,
                                         bias=bv_c[:, bass.ds(hh, 1)]).then_inc(o_free, 1)

                act.wait_ge(proj_free, 4 * PAIRS * (b + 1) + 4)
                if b:
                    act.wait_ge(merged, TC * b)
                split_qk(0)
                act.wait_ge(rms_step, 6 * b + 2)
                nc.scalar.activation(rk_rows[:, :], rk_rows[:, :], ACT.Sqrt).then_inc(rms_step, 1)
                nc.scalar.activation(rq[:, :], rq[:, :], ACT.Sqrt).then_inc(rms_step, 1)
                v_high(PAIRS * b)
                for c in range(TC):
                    exps(h0, 0, c)
                split_qk(1)

                def head_step(hh, e, last):
                    h = h0 + hh
                    more = not (last and e)
                    pT_high(h, 0)
                    pT_high(h, 1)
                    if more:
                        exps(h + 1, 1 - e, 0)
                    pT_high(h, 2)
                    if more:
                        exps(h + 1, 1 - e, 1)
                    pT_high(h, 3)
                    if more:
                        exps(h + 1, 1 - e, 2)
                    if not last:
                        act.wait_ge(s_done, TC * (h + 2))
                        split_qk(hh + 2)
                    if more:
                        exps(h + 1, 1 - e, 3)
                    store_o(h, e, hh)

                with act.Fori(0, PAIRS - 1) as p:
                    for e in range(2):
                        head_step(2 * p + e, e, False)
                    v_high(PAIRS * b + p + 1)
                for e in range(2):
                    head_step(HEADS - 2 + e, e, True)

                def oT_high(hh):
                    for e in range(2):
                        act.wait_ge(oT_used, (HEADS - 1) * b + hh + e + 1)
                        nc.scalar.activation(qk_hi[:, e, :], qs[:, hh + e, :], ACT.Copy).then_inc(oT_hi_ready, 1)
                act.wait_ge(o_free, HEADS * (b + 1) + 2)
                oT_high(0)
                oT_high(2)
                if b == 0:
                    split_xT(1)
                else:
                    gu_high(0, 0, P)
                    gu_high(0, 1, P)
                    for n in range(TC):
                        x1T_high(n)
                with act.Fori(2, PAIRS) as p:
                    oT_high(2 * p)
                for c in range(TC):
                    act.wait_ge(ln_var, TC * b + c + 1)
                    nc.scalar.activation(ln_rstd[:, c:c + 1], ln_rstd[:, c:c + 1], ACT.Sqrt).then_inc(ln_sqrt, 1)

            def hidden(n, par, j, b, rows):
                act.wait_ge(gate_done, n + 1)
                act.wait_ge(h_ready, n + 1)
                nc.scalar.activation(act_f[0:rows, par, :], bank[4 + 2 * par][0:rows, :], ACT.Silu).then_inc(silu_done, 1)
                act.wait_ge(h_done, n + 3)
                nc.scalar.activation(hid_hi[0:rows, j, b * S:(b + 1) * S], act_f[0:rows, par, :], ACT.Copy)\
                    .then_inc(h_hi_ready, 1)

            hidden(0, 0, *FIRST[0], P)
            hidden(1, 1, *FIRST[1], P)
            for n in range(TC, 2 * TC):
                x1T_high(n)
            hidden(2, 0, *FIRST[2], P)
            act.wait_ge(up_done, 3)
            gu_high(1, 0, P)
            hidden(3, 1, *FIRST[3], P)
            act.wait_ge(up_done, 4)
            gu_high(1, 1, P)
            with act.Fori(1, GROUPS - 1) as g:
                for jj in range(2):
                    for b in range(NB):
                        hidden(4 * g + 2 * jj + b, b, 2 * g + jj, b, P)
                    act.wait_ge(up_done, 4 * g + 2 * jj + 2)
                    gu_high(g + 1, jj, P)
            g = GROUPS - 1
            for b in range(NB):
                hidden(4 * g + b, b, 2 * g, b, P)
            act.wait_ge(up_done, 4 * g + 2)
            gu_high(GROUPS, 0, REST)
            for b in range(NB):
                hidden(4 * g + 2 + b, b, 2 * g + 1, b, P)

            def wd_high(b, j):
                rows = P if j < FC - 1 else REST
                n = FC * b + j
                act.wait_ge(w_eff, 6 * (j // 2) + 5 + j % 2)
                if n >= 2:
                    free_wd(act, n - 2)
                nc.scalar.activation(wd_hi[0:rows, n % 2, :], wd[0:rows, j, :], ACT.Copy).then_inc(wd_hi_ready, 1)

            wd_high(0, 0)
            wd_high(0, 1)
            for b in range(NB):
                hidden(4 * GROUPS + b, b, 2 * GROUPS, b, REST)
            for b in range(NB):
                for j in range(2 if b == 0 else 0, FC):
                    wd_high(b, j)
                    if b and j == 3:
                        roots_out(act, 0)
            roots_out(act, 1)

        @block.vector
        def _(dve):
            dve.sem_inc(s_free, 2)
            dve.sem_inc(pT_ready, 2)
            dve.sem_inc(h_done, 2)
            def w_high(i, part):
                nc.vector.tensor_copy(flat(w_hi[i], part), flat(w_stage[i], part)).then_inc(w_hi_ready[i], 1)

            def w_low(i, use, part):
                dve.wait_ge(w_hi_ready[i], 2 * use + 1 + part)
                op = nc.vector.tensor_tensor(flat(w_lo[i], part), flat(w_stage[i], part), f(flat(w_hi[i], part)),
                                             ALU.subtract)
                if part:
                    op.then_inc(w_ready[i], 1)

            def split_slab(i, use):
                dve.wait_ge(w_in[i], 16 * (use + 1))
                w_high(i, 0)
                w_high(i, 1)
                w_low(i, use, 0)
                w_low(i, use, 1)

            def split_xT(b):
                for k in range(KC):
                    dve.wait_ge(xT_hi_ready, KC * b + k + 1)
                    nc.vector.tensor_tensor(xT_lo[:, k, :], slots[:, 4 + k, :], f(xT_hi[:, k, :]), ALU.subtract)\
                        .then_inc(xT_ready, 1)

            def split_lora(t, t_f, block_lo, w, count, done):
                nc.vector.tensor_copy(t[0:LK, :, 0:w], t_f[0:LK, :, 0:w]).then_inc(done, 1)
                dve.wait_ge(done, count + 1)
                r = slice(32 * block_lo, 32 * block_lo + RANK)
                nc.vector.tensor_tensor(t[r, :, 0:w], t_f[r, :, 0:w], f(t[r, :, 0:w]), ALU.subtract).then_inc(done, 1)

            def x1T_low(n):
                dve.wait_ge(x1T_hi_ready, n + 1)
                at = slice((n % TC) * P, (n % TC + 1) * P)
                nc.vector.tensor_tensor(x1T_lo[n // TC][:, :, at],
                                        bank[4 + n % 2][:, :].rearrange("p (k t) -> p k t", k=KC),
                                        f(x1T_hi[n // TC][:, :, at]), ALU.subtract).then_inc(x1T_ready, 1)

            def fold_gu(g, w, first_bank):
                dve.wait_ge(gu_in, 80 * (g + 1))
                for i in range(2):
                    for half in range(2):
                        dve.wait_ge(fold_done, 6 * g + 2 * i + half + 1)
                        part = gu_stage[i][:, 2 * half:2 * half + 2, 0:w]
                        src = bank[first_bank + 2 * i + half][:, :].rearrange("p (k n) -> p k n", k=2)[:, :, 0:w]
                        nc.vector.tensor_tensor(part, src, part, ALU.add).then_inc(w_eff, 1)

            def fold_down(g, jj, rows):
                dve.wait_ge(fold_done, 6 * g + 5 + jj)
                part = wd[0:rows, bass.ds(2 * g + jj, 1), :].rearrange("p a n -> p (a n)")
                nc.vector.tensor_tensor(part, bank[jj][0:rows, :], part, ALU.add).then_inc(w_eff, 1)

            def gu_low(g, jj, w):
                for i in range(2):
                    dve.wait_ge(gu_hi_ready, 4 * g + 2 * jj + i + 1)
                    nc.vector.tensor_tensor(gu_lo[jj][i][:, :, 0:w], gu_stage[i][:, :, jj * P:jj * P + w],
                                            f(gu_hi[jj][i][:, :, 0:w]), ALU.subtract).then_inc(gu_ready, 1)

            def norm_rows(rows, n0, k0, src_bank, product, residual, loads=None):
                for c in range(TC):
                    dve.wait_ge(product, n0 + c + 1)
                    if residual is not None:
                        dve.wait_ge(residual, n0 + c + 1)
                    else:
                        dve.wait_ge(x1_in[c], 16 * loads)
                    nc.vector.tensor_tensor(rows[:, c, :], bank[src_bank + c][:, :], rows[:, c, :], ALU.add)\
                        .then_inc(ln_sum, 1)
                    dve.wait_ge(ln_sum, k0 + c + 1)
                    nc.vector.bn_stats(ln_stats[:, c, :], rows[:, c, :]).then_inc(ln_stat, 1)
                    dve.wait_ge(ln_stat, k0 + c + 1)
                    nc.vector.bn_aggr(ln_mv[:, c, :], ln_stats[:, c, :]).then_inc(ln_mean, 1)
                    dve.wait_ge(ln_mean, k0 + c + 1)
                    nc.vector.tensor_scalar(ln_rstd[:, c:c + 1], ln_mv[:, c, 1:2], LN_EPS, None, ALU.add)\
                        .then_inc(ln_var, 1)
                    if c:
                        norm_end(rows, k0, c - 1)
                norm_end(rows, k0, TC - 1)

            def norm_end(rows, k0, c):
                dve.wait_ge(ln_sqrt, k0 + c + 1)
                nc.vector.reciprocal(ln_rstd[:, c:c + 1], ln_rstd[:, c:c + 1]).then_inc(ln_inv, 1)
                dve.wait_ge(ln_inv, k0 + c + 1)
                nc.vector.tensor_scalar(rows[:, c, :], rows[:, c, :], ln_mv[:, c, 0:1], ln_rstd[:, c:c + 1],
                                        ALU.subtract, ALU.mult).then_inc(ln_done, 1)

            dve.wait_ge(const_in, 80)
            nc.vector.tensor_tensor(gqk[:, :], gqk[:, :], gk_c[:, :], ALU.mult).then_inc(bias_ready, 1)
            dve.wait_ge(bias_ready, 1)
            nc.vector.tensor_tensor(bqg[:, :], bq_c[:, :], gqk[:, :], ALU.mult).then_inc(bias_ready, 1)
            split_xT(0)
            for b in range(NB):
                h0 = HEADS * b
                if b:
                    dve.wait_ge(merged, TC * b)
                split_slab(0, use0(b, "project"))
                split_slab(1, use1(b, "project"))
                if b:
                    norm_rows(slots, 0, 0, 0, merged, res_ready)
                with dve.Fori(1, PAIRS) as p:
                    for i in range(2):
                        dve.wait_ge(proj_done, 4 * (PAIRS * b + p) - 2 + 2 * i)
                        split_slab(i, (use0, use1)[i](b, "project") + p)

                dve.wait_ge(proj_done, 4 * PAIRS * (b + 1) - 2)
                split_slab(0, use0(b, "attend"))
                dve.wait_ge(rms_sum, 2 * b + 1)
                nc.vector.tensor_scalar(rk_rows[:, :], bank[2][:, :], 1.0 / INNER, RMS_EPS, ALU.mult, ALU.add)\
                    .then_inc(rms_step, 1)
                dve.wait_ge(rms_sum, 2 * b + 2)
                nc.vector.tensor_scalar(rq[:, :], bank[3][:, 0:TC], 1.0 / INNER, RMS_EPS, ALU.mult, ALU.add)\
                    .then_inc(rms_step, 1)
                dve.wait_ge(rms_step, 6 * b + 4)
                nc.vector.reciprocal(rq[:, :], rq[:, :]).then_inc(rms_step, 1)
                nc.vector.reciprocal(rk_rows[:, :], rk_rows[:, :])
                dve.wait_ge(rms_step, 6 * b + 5)
                nc.vector.tensor_scalar(neg_rq[:, :], rq[:, :], -(DH ** -0.5), None, ALU.mult)
                nc.vector.tensor_scalar(rq[:, :], rq[:, :], DH ** -0.5, None, ALU.mult).then_inc(rms_step, 1)
                dve.wait_ge(rms_step, 6 * b + 6)

                def scale_scores(h, e, c):
                    s = TC * e + c
                    dve.wait_ge(s_done, TC * h + c + 1)
                    nc.vector.memset(carrier[:, s:s + 1], 0.0)
                    nc.vector.tensor_tensor_reduce(
                        out=slots[:, s, :], in0=bank[c % 2][:, :], in1=rk_rows[:, :], scale=1.0, scalar=FLOAT_MIN,
                        op0=ALU.mult, op1=ALU.max, accum_out=row_max[:, s:s + 1]).then_inc(s_free, 1)

                def normalise(h, e, half):
                    s = TC * e + 2 * half
                    dve.wait_ge(exp_done, TC * h + 2 * half + 2)
                    nc.vector.reciprocal(inv_sum[:, s:s + 2], row_sum[:, s:s + 2]).then_inc(inv_ready, 1)
                    dve.wait_ge(inv_ready, 2 * h + half + 1)
                    for c in range(2):
                        nc.vector.tensor_scalar(slots[:, s + c, :], slots[:, s + c, :], inv_sum[:, s + c:s + c + 1],
                                                None, ALU.mult).then_inc(p_ready, 1)

                def pT_low(h, j):
                    dve.wait_ge(pT_hi_ready, TC * h + j + 1)
                    nc.vector.tensor_tensor(pT_lo[:, j % 2, :], bank[2 + j % 2][:, :], f(pT_hi[:, j % 2, :]),
                                            ALU.subtract).then_inc(pT_ready, 1)

                def v_low(pair):
                    for half in range(2):
                        dve.wait_ge(v_hi_ready, 2 * pair + half + 1)
                        rows = slice(2 * half, 2 * half + 2)
                        nc.vector.tensor_tensor(v_lo[:, rows, :],
                                                bank[5 + half][:, :].rearrange("p (c n) -> p c n", c=2),
                                                f(v_hi[:, rows, :]), ALU.subtract).then_inc(v_ready, 1)

                v_low(PAIRS * b)
                if b:
                    dve.wait_ge(x1_out[0], 16 * TC)
                for c in range(TC):
                    scale_scores(h0, 0, c)
                for half in range(2):
                    normalise(h0, 0, half)

                def head_step(h, e, last, use=None, pair=None):
                    more = not (last and e)
                    pT_low(h, 0)
                    if more:
                        scale_scores(h + 1, 1 - e, 0)
                    if use is not None:
                        dve.wait_ge(w_in[0], 16 * (use + 1))
                        dve.wait_ge(v_done, 2 * pair)
                        w_high(0, 0)
                    pT_low(h, 1)
                    if more:
                        scale_scores(h + 1, 1 - e, 1)
                    if use is not None:
                        w_high(0, 1)
                    pT_low(h, 2)
                    if more:
                        scale_scores(h + 1, 1 - e, 2)
                    pT_low(h, 3)
                    if more:
                        scale_scores(h + 1, 1 - e, 3)
                        normalise(h + 1, 1 - e, 0)
                        normalise(h + 1, 1 - e, 1)

                with dve.Fori(0, PAIRS - 1) as p:
                    head_step(h0 + 2 * p, 0, False, use0(b, "attend") + 1 + p, PAIRS * b + p + 1)
                    head_step(h0 + 2 * p + 1, 1, False)
                    v_low(PAIRS * b + p + 1)
                head_step(h0 + HEADS - 2, 0, True)
                split_slab(0, use0(b, "merge"))
                head_step(h0 + HEADS - 1, 1, True)
                dve.wait_ge(pT_used, TC * HEADS * (b + 1) + 2)
                split_slab(1, use1(b, "merge"))
                if b == 0:
                    split_xT(1)
                else:
                    dve.wait_ge(la_in, 48)
                    split_lora(la, la_f, 2, D, 0, la_ready)
                    dve.wait_ge(gu_in, 80)
                    split_lora(lb, lb_f, 1, W2, 0, lb_ready)
                    fold_gu(0, W2, 4)
                    gu_low(0, 0, P)
                    gu_low(0, 1, P)
                    for n in range(TC):
                        x1T_low(n)
                with dve.Fori(1, PAIRS // 2) as p:
                    for i in range(2):
                        dve.wait_ge(oT_used, (HEADS - 1) * b + 4 * p + 2 * i)
                        split_slab(i, (use0, use1)[i](b, "merge") + p)

            norm_rows(slots, TC, TC, 0, merged, res_ready)

            def hidden(n, par, rows):
                dve.wait_ge(silu_done, n + 1)
                dve.wait_ge(up_done, n + 1)
                nc.vector.tensor_tensor(act_f[0:rows, par, :], bank[5 + 2 * par][0:rows, :], act_f[0:rows, par, :],
                                        ALU.mult).then_inc(h_done, 1)

            def prepare(g, w):
                dve.wait_ge(gu_in, 80 * (g + 1))
                dve.wait_ge(fold_done, 6 * g)
                split_lora(lb, lb_f, 1, w, 2 * g, lb_ready)
                fold_gu(g, w, 0)

            hidden(0, 0, P)
            hidden(1, 1, P)
            for n in range(TC, 2 * TC):
                x1T_low(n)
            hidden(2, 0, P)
            dve.wait_ge(wd_in, 32)
            fold_down(0, 0, P)
            fold_down(0, 1, P)
            prepare(1, W2)
            gu_low(1, 0, P)
            hidden(3, 1, P)
            fold_down(1, 0, P)
            fold_down(1, 1, P)
            gu_low(1, 1, P)
            with dve.Fori(1, GROUPS - 1) as g:
                for b in range(NB):
                    hidden(4 * g + b, b, P)
                prepare(g + 1, W2)
                gu_low(g + 1, 0, P)
                for b in range(NB):
                    hidden(4 * g + 2 + b, b, P)
                fold_down(g + 1, 0, P)
                fold_down(g + 1, 1, P)
                gu_low(g + 1, 1, P)
            g = GROUPS - 1
            for b in range(NB):
                hidden(4 * g + b, b, P)
            prepare(GROUPS, REST)
            gu_low(GROUPS, 0, REST)
            for b in range(NB):
                hidden(4 * g + 2 + b, b, P)
            fold_down(GROUPS, 0, REST)

            def wd_low(b, j):
                rows = P if j < FC - 1 else REST
                n = FC * b + j
                dve.wait_ge(wd_hi_ready, n + 1)
                nc.vector.tensor_tensor(wd_lo[0:rows, n % 2, :], wd[0:rows, j, :], f(wd_hi[0:rows, n % 2, :]),
                                        ALU.subtract).then_inc(wd_ready, 1)
            wd_low(0, 0)
            wd_low(0, 1)
            for b in range(NB):
                hidden(4 * GROUPS + b, b, REST)
            for j in range(2, FC):
                wd_low(0, j)
            for j in range(4):
                wd_low(1, j)
            norm_rows(x1_rows, 0, 2 * TC, 0, down_done, None, 3)
            for j in range(4, FC):
                wd_low(1, j)
            norm_rows(x1_rows, TC, 3 * TC, 4, down_done, None, 4)

        @block.tensor
        def _(pe):
            pe.sem_inc(pT_used, 2)
            pe.sem_inc(oT_used, 2)

            def mm3(dst, a, b_, first, last):
                nc.tensor.matmul(dst, a[0], b_[0], start=first, stop=False)
                nc.tensor.matmul(dst, a[0], b_[1], start=False, stop=False)
                return nc.tensor.matmul(dst, a[1], b_[0], start=False, stop=last)

            def transpose_x1(n):
                pe.wait_ge(x1_in[n % 4], 16 * (n // 4 + 1))
                for k in range(KC):
                    last = nc.tensor.transpose(bank[4 + n % 2][:, k * P:(k + 1) * P],
                                               x1_rows[:, n % 4, k * P:(k + 1) * P], ident[:, :])
                last.then_inc(x1T_done, 1)

            def fold_gu(g, w, first_bank):
                pe.wait_ge(lb_ready, 2 * g + 2)
                for i in range(2):
                    for half in range(2):
                        for k in range(2):
                            kc = 2 * half + k
                            last = nc.tensor.matmul(
                                bank[first_bank + 2 * i + half][:, k * W2:k * W2 + w],
                                la[0:LK, i, kc * P:(kc + 1) * P], lb[0:LK, i, 0:w], start=True, stop=True)
                        last.then_inc(fold_done, 1)

            def fold_down(jj, rows):
                nc.tensor.matmul(bank[jj][0:rows, :], lb[0:LK, 2, jj * P:jj * P + rows], la[0:LK, 2, :],
                                 start=True, stop=True).then_inc(fold_done, 1)

            pe.wait_ge(xT_ready, KC)
            for b in range(NB):
                h0 = HEADS * b
                if b:
                    pe.wait_ge(xT_ready, KC * (b + 1))
                    pe.wait_ge(o_free, HEADS * b + 2)
                    pe.wait_ge(v_ready, 2 * PAIRS * b)
                with pe.Fori(0, PAIRS) as p:
                    for u in range(4):
                        unit = 4 * (b * PAIRS + p) + u
                        i, e = u // 2, u % 2
                        if e == 0:
                            pe.wait_ge(w_ready[i], (use0, use1)[i](b, "project") + p + 1)
                        pe.wait_ge(proj_free, unit + 1)
                        for k in range(KC):
                            cols = slice(e * DH, (e + 1) * DH)
                            last = mm3(bank[4 + u][:, :], (w_hi[i][:, k, cols], w_lo[i][:, k, cols]),
                                       (xT_hi[:, k, :], xT_lo[:, k, :]), k == 0, k == KC - 1)
                        last.then_inc(proj_done, 1)

                def values(pair, half, chunks=(0, 1)):
                    for c in chunks:
                        at = (2 * half + c) * P
                        for k in range(KC):
                            last = mm3(bank[5 + half][:, c * W2:(c + 1) * W2],
                                       (xT_hi[:, k, at:at + P], xT_lo[:, k, at:at + P]),
                                       (w_hi[0][:, k, :], w_lo[0][:, k, :]), k == 0, k == KC - 1)
                    if c:
                        last.then_inc(v_done, 1)

                def scores(h, c):
                    if c == 0:
                        pe.wait_ge(qk_ready, 2 * h + 2)
                    pe.wait_ge(s_free, TC * h + c + 1)
                    mm3(bank[c % 2][:, :], [t[:, 0, c * P:(c + 1) * P] for t in (qk_hi, qk_lo)],
                        [t[:, 1, :] for t in (qk_hi, qk_lo)], True, True).then_inc(s_done, 1)

                def transpose_p(h, e, j):
                    if j == 0:
                        pe.wait_ge(p_ready, TC * h + TC)
                    pe.wait_ge(pT_ready, TC * h + j + 1)
                    for c in range(TC):
                        last = nc.tensor.transpose(bank[2 + j % 2][:, c * P:(c + 1) * P],
                                                   slots[:, TC * e + c, j * P:(j + 1) * P], ident[:, :])
                    last.then_inc(pT_done, 1)

                def weighted(h, e, j):
                    if j == 0:
                        pe.wait_ge(o_free, h + 1)
                    pe.wait_ge(pT_ready, TC * h + j + 3)
                    cols = slice(e * DH, (e + 1) * DH)
                    mm3(bank[O_BANK[e]][:, :], (v_hi[:, j, cols], v_lo[:, j, cols]),
                        (pT_hi[:, j % 2, :], pT_lo[:, j % 2, :]), j == 0, j == TC - 1).then_inc(pT_used, 1)

                pe.wait_ge(proj_free, 4 * PAIRS * (b + 1) + 4)
                pe.wait_ge(w_ready[0], use0(b, "attend") + 1)
                values(PAIRS * b, 0)
                pe.wait_ge(sq_added, 4 * PAIRS * (b + 1) + 2)
                pe.wait_ge(ones_ready, b + 1)
                nc.tensor.matmul(bank[2][:, :], ones, slots[:, 5, :], start=True, stop=True).then_inc(rms_sum, 1)
                for c in range(TC):
                    last = nc.tensor.matmul(bank[3][:, c:c + 1], slots[:, 4, c * P:(c + 1) * P], ones[:, 0:1],
                                            start=True, stop=True)
                last.then_inc(rms_sum, 1)
                values(PAIRS * b, 1)
                if b == 0:
                    pe.wait_ge(ident_ready, 1)
                else:
                    pe.wait_ge(ln_sum, TC)
                for c in range(TC):
                    scores(h0, c)

                def head_step(h, e, last, v_needed, first_v, second_v):
                    more = not (last and e)

                    def more_scores(c):
                        if more:
                            scores(h + 1, c)
                    transpose_p(h, e, 0)
                    more_scores(0)
                    transpose_p(h, e, 1)
                    more_scores(1)
                    if e == 0:
                        pe.wait_ge(v_ready, v_needed)
                    weighted(h, e, 0)
                    transpose_p(h, e, 2)
                    more_scores(2)
                    weighted(h, e, 1)
                    transpose_p(h, e, 3)
                    more_scores(3)
                    weighted(h, e, 2)
                    first_v()
                    weighted(h, e, 3)
                    second_v()

                with pe.Fori(0, PAIRS - 1) as p:
                    for e in range(2):
                        pair = PAIRS * b + p

                        def first_v():
                            if e == 0:
                                pe.wait_ge(w_ready[0], use0(b, "attend") + p + 2)
                            pe.wait_ge(v_ready, 2 * pair + e + 1)
                            values(pair + 1, e, (0,))
                        head_step(h0 + 2 * p + e, e, False, 2 * pair + 2, first_v, lambda: values(pair + 1, e, (1,)))
                for e in range(2):
                    head_step(h0 + HEADS - 2 + e, e, True, 2 * PAIRS * (b + 1), lambda: None, lambda: None)

                def merge_head(hh, m, first, final):
                    i, e = m // 2, m % 2
                    pe.wait_ge(oT_ready, h0 + hh + 1)
                    rhs = [t[:, 2 * e:2 * e + 2, :].rearrange("p k n -> p (k n)") for t in (w_hi[i], w_lo[i])]
                    for c in range(TC):
                        last = mm3(bank[c][:, :], [t[:, e, c * P:(c + 1) * P] for t in (qk_hi, qk_lo)], rhs, first, final)
                        if final:
                            last.then_inc(merged, 1)
                    if not final:
                        last.then_inc(oT_used, 1)

                def merge_four(p, first, final):
                    for m in range(4):
                        if m % 2 == 0:
                            pe.wait_ge(w_ready[m // 2], (use0, use1)[m // 2](b, "merge") + p + 1)
                        merge_head(4 * p + m, m, first and m == 0, final and m == 3)

                pe.wait_ge(s_free, TC * HEADS * (b + 1) + 2)
                pe.wait_ge(pT_ready, TC * HEADS * (b + 1) + 2)
                merge_four(0, True, False)
                if b == NB - 1:
                    pe.wait_ge(la_ready, 2)
                    pe.wait_ge(o_free, HEADS * NB + 2)
                    pe.wait_ge(v_ready, 2 * PAIRS * NB)
                    fold_gu(0, W2, 4)
                    for n in range(TC):
                        if n < 2:
                            pe.wait_ge(w_eff, n + 1)
                        else:
                            pe.wait_ge(x1T_ready, n - 1)
                        transpose_x1(n)
                with pe.Fori(1, PAIRS // 2 - 1) as p:
                    merge_four(p, False, False)
                merge_four(PAIRS // 2 - 1, False, True)

            def gate_up(n, par, j, jj, b, rows):
                pe.wait_ge(h_done, n + 1)
                for i in range(2):
                    pe.wait_ge(gu_ready, 2 * j + i + 1)
                    for k in range(KC):
                        last = mm3(bank[4 + 2 * par + i][0:rows, :],
                                   (gu_hi[jj][i][:, k, 0:rows], gu_lo[jj][i][:, k, 0:rows]),
                                   (x1T_hi[b][:, k, :], x1T_lo[b][:, k, :]), k == 0, k == KC - 1)
                    last.then_inc((gate_done, up_done)[i], 1)

            pe.wait_ge(x1T_ready, TC)
            pe.wait_ge(w_eff, 4)
            gate_up(0, 0, 0, 0, 0, P)
            gate_up(1, 1, 1, 1, 0, P)
            pe.wait_ge(h_done, 3)
            for n in range(TC, 2 * TC):
                if n >= TC + 2:
                    pe.wait_ge(x1T_ready, n - 1)
                transpose_x1(n)
            pe.wait_ge(x1T_ready, 2 * TC)
            gate_up(2, 0, 0, 0, 1, P)
            pe.wait_ge(ln_sum, 2 * TC)
            fold_down(0, P)
            fold_down(1, P)
            pe.wait_ge(w_eff, 6)
            fold_gu(1, W2, 0)
            gate_up(3, 1, 1, 1, 1, P)
            pe.wait_ge(w_eff, 8)
            fold_down(0, P)
            fold_down(1, P)

            def group(g, next_w, next_down):
                for b in range(NB):
                    gate_up(4 * g + b, b, 2 * g, 0, b, P)
                pe.wait_ge(w_eff, 6 * g + 6)
                fold_gu(g + 1, next_w, 0)
                for b in range(NB):
                    gate_up(4 * g + 2 + b, b, 2 * g + 1, 1, b, P)
                pe.wait_ge(w_eff, 6 * g + 8)
                for jj, rows in enumerate(next_down):
                    fold_down(jj, rows)
            with pe.Fori(1, GROUPS - 1) as g:
                group(g, W2, (P, P))
            group(GROUPS - 1, REST, (REST,))
            for b in range(NB):
                gate_up(4 * GROUPS + b, b, 2 * GROUPS, 0, b, REST)

            pe.wait_ge(w_eff, 6 * GROUPS + 5)
            for b in range(NB):
                if b:
                    pe.wait_ge(h_done, 4 * GROUPS + NB + 2)
                for j in range(FC):
                    n = FC * b + j
                    rows = P if j < FC - 1 else REST
                    pe.wait_ge(wd_ready, n + 1)
                    pe.wait_ge(h_ready, (4 * GROUPS + b if j == FC - 1 else 4 * (FC // 2) - 1 if j > 1 else 3) + 3)
                    for c in range(TC):
                        at = b * S + c * P
                        last = mm3(bank[4 * b + c][:, :],
                                   (hid_hi[0:rows, j, at:at + P], hid_lo[0:rows, j, at:at + P]),
                                   (wd_hi[0:rows, n % 2, :], wd_lo[0:rows, n % 2, :]), j == 0, j == FC - 1)
                        if j == FC - 1:
                            last.then_inc(down_done, 1)
                    if j < FC - 1:
                        last.then_inc(wd_used, 1)


def arranged(inputs):
    import numpy as np
    i = {k.replace("L0_", ""): np.asarray(v) for k, v in inputs.items()}
    x = i["attn_hidden_states"].reshape(NB * S, D)

    def by_head(v):
        return v.reshape(HEADS, DH).T
    return {
        "xT": x.T, "x": x, "wq": i["attn_Wq"], "wk": i["attn_Wk"], "wv": i["attn_Wv"], "wo": i["attn_Wo"],
        "bq": by_head(i["attn_bq"]), "bk": by_head(i["attn_bk"]), "bv": by_head(i["attn_bv"]), "bo": i["attn_bo"],
        "gq": by_head(i["attn_gq"]), "gk": by_head(i["attn_gk"]),
        "gate_w": i["ffn_gate_w"].T, "up_w": i["ffn_up_w"].T, "down_w": i["ffn_down_w"].T,
        "lora_a": np.stack([i["ffn_gate_a"], i["ffn_up_a"], i["ffn_down_b"].T], 1),
        "lora_b": np.stack([i["ffn_gate_b"].T, i["ffn_up_b"].T, i["ffn_down_a"]], 1),
    }


def kernel(**inputs):
    import numpy as np
    import concourse.bacc as bacc
    from concourse.bass_utils import run_bass_kernel_spmd

    nc = bacc.Bacc("TRN2", target_bir_lowering=False, num_devices=1)
    arrays, args = {}, []
    for name, a in arranged(inputs).items():
        arrays[name] = np.ascontiguousarray(a)
        args.append(nc.dram_tensor(name, a.shape, mybir.dt.from_np(a.dtype), kind="ExternalInput").ap())
    args.append(nc.dram_tensor("x1_scratch", (NB * S, D), F32, kind="Internal").ap())
    args.append(nc.dram_tensor("out", (NB * S, D), F32, kind="ExternalOutput").ap())
    layer_kernel(nc, *args)
    r = run_bass_kernel_spmd(nc, [arrays], core_ids=[0])
    return r.results[0]["out"].reshape(NB, S, D)
```

```python
import concourse.bass as bass
from concourse import mybir
from contextlib import ExitStack

F32 = mybir.dt.float32
F32R = mybir.dt.float32r
ALU = mybir.AluOpType
ACT = mybir.ActivationFunctionType
AX = mybir.AxisListType

P = 128
NB, S, D = 2, 512, 512
HEADS, DH = 32, 128
INNER = HEADS * DH
FF, RANK = 1376, 16
KC = D // P
TC = S // P
PAIRS = HEADS // 2
W2 = 2 * DH
RMS_EPS, LN_EPS = 1e-6, 1e-5
FLOAT_MIN = -3.4028234e38
GROUPS = FF // W2
REST = FF - GROUPS * W2
FC = GROUPS * 2 + 1
FIRST = ((0, 0), (1, 0), (0, 1), (1, 1))
LK = 80


def layer_kernel(nc, xT, x, wq, wk, wv, wo, bq, bk, bv, bo, gq, gk,
                 gate_w, up_w, down_w, lora_a, lora_b, x1_dram, out):
    ctx = ExitStack()
    with ctx:
        def sem(name):
            return ctx.enter_context(nc.semaphore(name))

        O_BANK = (4, 7)
        bank = [ctx.enter_context(nc.psum_tensor(f"bank{i}", [P, 512], F32)) for i in range(8)]

        def const(name, shape):
            return ctx.enter_context(nc.sbuf_tensor(name, shape, F32))

        ident = const("ident", [P, P])
        bq_c = const("bq_c", [P, HEADS])
        bk_c = const("bk_c", [P, HEADS])
        bv_c = const("bv_c", [P, HEADS])
        gqk = const("gqk", [P, HEADS])
        gk_c = const("gk_c", [P, HEADS])
        bqg = const("bqg", [P, HEADS])
        eps = const("eps", [P, 2])
        rms = const("rms", [P, 2 * TC])
        rq = const("rq", [P, TC])
        neg_rq = const("neg_rq", [P, TC])
        row_max = const("row_max", [P, 8])
        neg_max = const("neg_max", [P, 8])
        carrier = const("carrier", [P, 8])
        row_sum = const("row_sum", [P, 8])
        inv_sum = const("inv_sum", [P, 8])
        ln_stats = const("ln_stats", [P, TC, 6])
        ln_mv = const("ln_mv", [P, TC, 2])
        ln_rstd = const("ln_rstd", [P, TC])

        with ExitStack() as region:
            def sa(name, shape, dt=F32):
                return region.enter_context(nc.sbuf_tensor(name, shape, dt))
            ks = sa("ks", [P, HEADS, S])
            qs = sa("qs", [P, HEADS, S])
            w_stage = [sa(f"w_stage{i}", [P, KC, W2]) for i in range(2)]
            slots = sa("slots", [P, 8, S])
            xT_hi = sa("xT_hi", [P, KC, S], F32R)
            xT_lo = sa("xT_lo", [P, KC, S], F32R)
            w_hi = [sa(f"w_hi{i}", [P, KC, W2], F32R) for i in range(2)]
            w_lo = [sa(f"w_lo{i}", [P, KC, W2], F32R) for i in range(2)]
            qk_hi = sa("qk_hi", [P, 2, S], F32R)
            qk_lo = sa("qk_lo", [P, 2, S], F32R)
            pT_hi = sa("pT_hi", [P, 2, S], F32R)
            pT_lo = sa("pT_lo", [P, 2, S], F32R)
            rk_rows = sa("rk_rows", [P, S])
            bo_rows = sa("bo_rows", [P, D])
        v_hi, v_lo = w_hi[1], w_lo[1]
        ones = bo_rows[:, 0:P]

        with ExitStack() as region:
            def sf(name, shape, dt=F32):
                return region.enter_context(nc.sbuf_tensor(name, shape, dt))
            x1_rows = sf("x1_rows", [P, 4, D])
            lb_f = sf("lb_f", [P, 3, W2])
            la = sf("la", [P, 3, D], F32R)
            lb = sf("lb", [P, 3, W2], F32R)
            gu_stage = [sf(f"gu_stage{i}", [P, KC, W2]) for i in range(2)]
            gu_hi = [[sf(f"gu_hi{j}{i}", [P, KC, P], F32R) for i in range(2)] for j in range(2)]
            gu_lo = [[sf(f"gu_lo{j}{i}", [P, KC, P], F32R) for i in range(2)] for j in range(2)]
            x1T_hi = [sf("x1T_hi0", [P, KC, S], F32R)]
            x1T_lo = [sf("x1T_lo0", [P, KC, S], F32R)]
            x1T_hi.append(sf("x1T_hi1", [P, KC, S], F32R))
            x1T_lo.append(sf("x1T_lo1", [P, KC, S], F32R))
            wd = sf("wd", [P, FC, D])
            wd_hi = sf("wd_hi", [P, 2, D], F32R)
            wd_lo = sf("wd_lo", [P, 2, D], F32R)
            hid_hi = sf("hid_hi", [P, FC, NB * S], F32R)
            hid_lo = sf("hid_lo", [P, FC, NB * S], F32R)
            act_f = sf("act_f", [P, 2, S])
        la_f = x1_rows[:, 0:3, :]

        def f(ap):
            return ap.bitcast(F32)

        const_in = sem("const_in")
        ident_zero = sem("ident_zero")
        ident_ready = sem("ident_ready")
        ones_ready = sem("ones_ready")
        eps_ready = sem("eps_ready")
        bias_ready = sem("bias_ready")
        x_in = sem("x_in")
        xT_hi_ready = sem("xT_hi_ready")
        xT_ready = sem("xT_ready")
        w_in = [sem(f"w_in{i}") for i in range(2)]
        w_hi_ready = [sem(f"w_hi_ready{i}") for i in range(2)]
        w_ready = [sem(f"w_ready{i}") for i in range(2)]
        acc_zero = sem("acc_zero")
        proj_done = sem("proj_done")
        squared = sem("squared")
        proj_free = sem("proj_free")
        sq_added = sem("sq_added")
        rms_sum = sem("rms_sum")
        rms_step = sem("rms_step")
        rk_spread = sem("rk_spread")
        rk_ready = sem("rk_ready")
        qk_hi_ready = sem("qk_hi_ready")
        k_ready = sem("k_ready")
        q_ready = sem("q_ready")
        s_done = sem("s_done")
        s_free = sem("s_free")
        max_ready = sem("max_ready")
        exp_done = sem("exp_done")
        inv_ready = sem("inv_ready")
        p_ready = sem("p_ready")
        pT_done = sem("pT_done")
        pT_hi_ready = sem("pT_hi_ready")
        pT_ready = sem("pT_ready")
        pT_used = sem("pT_used")
        o_free = sem("o_free")
        v_done = sem("v_done")
        v_hi_ready = sem("v_hi_ready")
        v_ready = sem("v_ready")
        oT_hi_ready = sem("oT_hi_ready")
        oT_ready = sem("oT_ready")
        oT_used = sem("oT_used")
        res_in = sem("res_in")
        res_ready = sem("res_ready")
        merged = sem("merged")
        ln_sum = sem("ln_sum")
        ln_stat = sem("ln_stat")
        ln_mean = sem("ln_mean")
        ln_sqrt = sem("ln_sqrt")
        ln_inv = sem("ln_inv")
        ln_done = sem("ln_done")
        x1_out = [sem(f"x1_out{i}") for i in range(NB)]
        la_in = sem("la_in")
        lora_zero = sem("lora_zero")
        la_ready = sem("la_ready")
        gu_in = sem("gu_in")
        lb_ready = sem("lb_ready")
        fold_done = sem("fold_done")
        w_eff = sem("w_eff")
        gu_hi_ready = sem("gu_hi_ready")
        gu_ready = sem("gu_ready")
        wd_in = sem("wd_in")
        x1_in = [sem(f"x1_in{i}") for i in range(4)]
        x1T_done = sem("x1T_done")
        x1T_hi_ready = sem("x1T_hi_ready")
        x1T_ready = sem("x1T_ready")
        gate_done = sem("gate_done")
        up_done = sem("up_done")
        silu_done = sem("silu_done")
        h_done = sem("h_done")
        h_hi_ready = sem("h_hi_ready")
        h_ready = sem("h_ready")
        wd_hi_ready = sem("wd_hi_ready")
        wd_ready = [sem(f"wd_ready{b}") for b in range(NB)]
        wd_used = sem("wd_used")
        down_done = sem("down_done")
        out_done = [sem(f"out_done{i}") for i in range(4)]

        USES = (2 * PAIRS + PAIRS // 2, PAIRS + PAIRS // 2)

        def use0(b, phase):
            return b * USES[0] + {"project": 0, "attend": PAIRS, "merge": 2 * PAIRS}[phase]

        def use1(b, phase):
            return b * USES[1] + {"project": 0, "merge": PAIRS}[phase]

        def free_wd(eng, n):
            if n % FC == FC - 1:
                eng.wait_ge(down_done, TC * (n // FC + 1))
            else:
                eng.wait_ge(wd_used, (FC - 1) * (n // FC) + n % FC + 1)

        def ln_root(act, k0, c):
            act.wait_ge(ln_mean, k0 + c + 1)
            nc.scalar.activation(ln_rstd[:, c:c + 1], ln_mv[:, c, 1:2], ACT.Sqrt, bias=eps[:, 1:2]).then_inc(ln_sqrt, 1)

        def roots_out(act, b):
            for c in range(TC):
                ln_root(act, TC * (NB + b), c)
                if c:
                    store_out(act, b, c - 1)
            store_out(act, b, TC - 1)

        def store_out(act, b, c):
            act.wait_ge(ln_done, TC * (NB + b) + c + 1)
            act.dma_start(out[(TC * b + c) * P:(TC * b + c + 1) * P, :], x1_rows[:, c, :]).then_inc(out_done[c], 16)

        def wd_low(eng, ops, b, j):
            rows = P if j < FC - 1 else REST
            n = FC * b + j
            eng.wait_ge(wd_hi_ready, n + 1)
            ops.tensor_tensor(wd_lo[0:rows, n % 2, :], wd[0:rows, j, :], f(wd_hi[0:rows, n % 2, :]),
                              ALU.subtract).then_inc(wd_ready[b], 1)

        def x1T_bank(n):
            return 4 + n % 2 if n < TC else n - TC

        def flat(t, part):
            half = KC * W2 // 2
            return t[:, :, :].rearrange("p k n -> p (k n)")[:, part * half:(part + 1) * half]

        block = ctx.enter_context(nc.Block())

        @block.sync
        def _(sp):
            wq_v, wk_v, wv_v, gate_v, up_v = (w.rearrange("(k p) n -> p k n", p=P)
                                              for w in (wq, wk, wv, gate_w, up_w))
            wo_v = wo.rearrange("(h p) n -> p h n", p=P)
            x1_v = x1_dram.rearrange("(c p) d -> p c d", p=P)

            def load_w(i, use, src):
                sp.wait_ge(w_ready[i], use)
                sp.dma_start(w_stage[i][:, :, :], src).then_inc(w_in[i], 16)

            def load_qk(b, p):
                load_w(0, use0(b, "project") + p, wq_v[:, :, bass.ds(p * W2, W2)])
                load_w(1, use1(b, "project") + p, wk_v[:, :, bass.ds(p * W2, W2)])

            def load_wo(b, p):
                for i, use in ((0, use0(b, "merge") + p), (1, use1(b, "merge") + p)):
                    sp.wait_ge(w_ready[i], use)
                    sp.dma_start(w_stage[i][:, :, :].rearrange("p k n -> p (k n)").rearrange("p (h n) -> p h n", h=2),
                                 wo_v[:, bass.ds(4 * p + 2 * i, 2), :]).then_inc(w_in[i], 16)

            def load_xT(b):
                sp.dma_start(slots[:, 4:8, :], xT[:, b * S:(b + 1) * S].rearrange("(k p) t -> p k t", p=P))\
                    .then_inc(x_in, 16)

            def load_gu(g, w):
                sp.dma_start(gu_stage[0][:, :, 0:w], gate_v[:, :, bass.ds(g * W2, w)]).then_inc(gu_in, 16)
                sp.dma_start(gu_stage[1][:, :, 0:w], up_v[:, :, bass.ds(g * W2, w)]).then_inc(gu_in, 16)
                for r in range(3):
                    sp.dma_start(lb_f[32 * r:32 * r + RANK, :, 0:w], lora_b[:, :, bass.ds(g * W2, w)])\
                        .then_inc(gu_in, 16)

            def load_x1(n):
                sp.dma_start(x1_rows[:, n % 4, :], x1_v[:, n, :]).then_inc(x1_in[n % 4], 16)

            load_xT(0)
            sp.dma_start(w_stage[0][:, :, :], wq_v[:, :, 0:W2]).then_inc(w_in[0], 16)
            sp.dma_start(w_stage[1][:, :, :], wk_v[:, :, 0:W2]).then_inc(w_in[1], 16)
            for dst, src in ((bq_c, bq), (bk_c, bk), (bv_c, bv), (gqk, gq), (gk_c, gk)):
                sp.dma_start(dst[:, :], src).then_inc(const_in, 16)
            for b in range(NB):
                if b:
                    load_qk(b, 0)
                with sp.Fori(1, PAIRS) as p:
                    load_qk(b, p)
                with sp.Fori(0, PAIRS) as p:
                    load_w(0, use0(b, "attend") + p, wv_v[:, :, bass.ds(p * W2, W2)])
                load_wo(b, 0)
                sp.wait_ge(pT_done, TC * HEADS * (b + 1))
                if b == 0:
                    load_xT(1)
                sp.dma_start(slots[:, 0:TC, :], x[b * S:(b + 1) * S, :].rearrange("(c p) d -> p c d", p=P))\
                    .then_inc(res_in, 16)
                sp.dma_start(bo_rows[:, :], bo.partition_broadcast(P)).then_inc(res_in, 16)
                if b == NB - 1:
                    sp.wait_ge(lora_zero, 2)
                    for r in range(3):
                        sp.dma_start(la_f[32 * r:32 * r + RANK, :, :], lora_a).then_inc(la_in, 16)
                    load_gu(0, W2)
                    sp.wait_ge(la_ready, 2)
                    sp.wait_ge(x1_out[0], 16 * TC)
                    for n in range(TC):
                        load_x1(n)
                with sp.Fori(1, PAIRS // 2) as p:
                    load_wo(b, p)

            sp.wait_ge(gu_ready, 4)
            sp.wait_ge(lb_ready, 2)
            load_gu(1, W2)
            sp.wait_ge(merged, TC * NB)
            sp.dma_start(wd[:, 0:2 * GROUPS, :], down_w[0:GROUPS * W2, :].rearrange("(j p) n -> p j n", p=P))\
                .then_inc(wd_in, 16)
            sp.dma_start(wd[0:REST, 2 * GROUPS, :], down_w[GROUPS * W2:FF, :]).then_inc(wd_in, 16)
            with sp.Fori(2, GROUPS) as g:
                sp.wait_ge(gu_ready, 4 * g)
                load_gu(g, W2)
            sp.wait_ge(gu_ready, 4 * GROUPS)
            sp.wait_ge(lb_ready, 2 * GROUPS)
            load_gu(GROUPS, REST)
            sp.wait_ge(x1_out[1], 16 * TC)
            for n in range(TC, 2 * TC):
                sp.wait_ge(out_done[n % 4], 16)
                load_x1(n)
            for i in range(4):
                sp.wait_ge(out_done[i], 32)

        @block.gpsimd
        def _(pool):
            pool.sem_inc(sq_added, 2)
            pool.sem_inc(h_ready, 2)
            pool.memset(ident[:, :], 0.0).then_inc(ident_zero, 1)
            pool.memset(ones, 1.0).then_inc(ones_ready, 1)
            pool.memset(eps[:, 0:1], RMS_EPS).then_inc(eps_ready, 1)
            pool.memset(eps[:, 1:2], LN_EPS).then_inc(eps_ready, 1)
            pool.wait_ge(ident_zero, 1)
            pool.affine_select(out=ident[:, :], in_=ident[:, :], compare_op=ALU.not_equal, fill=1.0,
                               base=0, pattern=[[-1, P]], channel_multiplier=1).then_inc(ident_ready, 1)
            for b in range(NB):
                h0 = HEADS * b
                pool.wait_ge(xT_ready, KC * (b + 1))
                pool.memset(slots[:, 4:6, :], 0.0).then_inc(acc_zero, 1)
                if b:
                    pool.memset(ones, 1.0).then_inc(ones_ready, 1)
                pool.wait_ge(acc_zero, b + 1)
                with pool.Fori(0, PAIRS) as p:
                    for u in range(4):
                        unit = 4 * (b * PAIRS + p) + u
                        pool.wait_ge(squared, unit + 1)
                        pool.wait_ge(sq_added, unit + 2)
                        acc = slots[:, 4 + u // 2, :]
                        nc.gpsimd.tensor_tensor(acc, acc, slots[:, 6 + u % 2, :], ALU.add).then_inc(sq_added, 1)

                def k_low(h, hh):
                    pool.wait_ge(qk_hi_ready, 2 * h + 1)
                    nc.gpsimd.tensor_tensor(qk_lo[:, 1, :], ks[:, hh, :], f(qk_hi[:, 1, :]), ALU.subtract)\
                        .then_inc(k_ready, 1)

                def neg_maxima(h, e, c):
                    s = TC * e + c
                    pool.wait_ge(s_free, TC * h + c + 3)
                    nc.gpsimd.tensor_tensor(neg_max[:, s:s + 1], row_max[:, s:s + 1], neg_rq[:, c:c + 1],
                                            ALU.mult).then_inc(max_ready, 1)

                k_low(h0, 0)
                pool.wait_ge(rms_step, 4 * b + 4)
                for c in range(TC):
                    neg_maxima(h0, 0, c)
                k_low(h0 + 1, 1)
                with pool.Fori(0, PAIRS - 1) as p:
                    for e in range(2):
                        hh = 2 * p + e
                        for c in range(TC):
                            neg_maxima(h0 + hh + 1, 1 - e, c)
                            if e == 0 and c < 2:
                                pool.wait_ge(w_hi_ready[0], 2 * (use0(b, "attend") + p + 1) + c + 1)
                                op = nc.gpsimd.tensor_tensor(flat(w_lo[0], c), flat(w_stage[0], c),
                                                             f(flat(w_hi[0], c)), ALU.subtract)
                                if c == 1:
                                    op.then_inc(w_ready[0], 1)
                        k_low(h0 + hh + 2, hh + 2)
                for c in range(TC):
                    neg_maxima(h0 + HEADS - 1, 1, c)

                def oT_low(hh):
                    for e in range(2):
                        pool.wait_ge(oT_hi_ready, h0 + hh + e + 1)
                        nc.gpsimd.tensor_tensor(qk_lo[:, e, :], qs[:, hh + e, :], f(qk_hi[:, e, :]),
                                                ALU.subtract).then_inc(oT_ready, 1)
                if b == NB - 1:
                    pool.wait_ge(s_done, TC * HEADS * NB)
                    pool.memset(la_f, 0.0).then_inc(lora_zero, 1)
                    pool.memset(lb_f[:, :, :], 0.0).then_inc(lora_zero, 1)
                oT_low(0)
                oT_low(2)
                pool.wait_ge(res_in, 32 * (b + 1))
                for c in range(TC):
                    nc.gpsimd.tensor_tensor(slots[:, c, :], slots[:, c, :], bo_rows[:, :], ALU.add)\
                        .then_inc(res_ready, 1)
                with pool.Fori(2, PAIRS) as p:
                    oT_low(2 * p)
                for c in range(TC):
                    pool.wait_ge(ln_done, TC * b + c + 1)
                    pool.dma_start(x1_dram[(TC * b + c) * P:(TC * b + c + 1) * P, :], slots[:, c, :])\
                        .then_inc(x1_out[b], 16)

            def hid_low(n, par, j, b, rows):
                pool.wait_ge(h_hi_ready, n + 1)
                nc.gpsimd.tensor_tensor(hid_lo[0:rows, j, b * S:(b + 1) * S], act_f[0:rows, par, :],
                                        f(hid_hi[0:rows, j, b * S:(b + 1) * S]), ALU.subtract).then_inc(h_ready, 1)
            for n, (j, b) in enumerate(FIRST):
                hid_low(n, n % 2, j, b, P)
            with pool.Fori(1, GROUPS) as g:
                for jj in range(2):
                    for b in range(NB):
                        hid_low(4 * g + 2 * jj + b, b, 2 * g + jj, b, P)
            for b in range(NB):
                hid_low(4 * GROUPS + b, b, 2 * GROUPS, b, REST)
            for j in range(FC):
                wd_low(pool, nc.gpsimd, 1, j)

        @block.scalar
        def _(act):
            act.sem_inc(proj_free, 4)
            act.sem_inc(o_free, 2)

            def split_xT(b):
                act.wait_ge(x_in, 16 * (b + 1))
                for k in range(KC):
                    nc.scalar.activation(xT_hi[:, k, :], slots[:, 4 + k, :], ACT.Copy).then_inc(xT_hi_ready, 1)

            def x1T_high(n):
                act.wait_ge(x1T_done, n + 1)
                nc.scalar.activation(x1T_hi[n // TC][:, :, (n % TC) * P:(n % TC + 1) * P],
                                     bank[x1T_bank(n)][:, :].rearrange("p (k t) -> p k t", k=KC), ACT.Copy)\
                    .then_inc(x1T_hi_ready, 1)

            def gu_high(g, jj, w):
                act.wait_ge(w_eff, 6 * g + 4)
                for i in range(2):
                    nc.scalar.activation(gu_hi[jj][i][:, :, 0:w], gu_stage[i][:, :, jj * P:jj * P + w], ACT.Copy)\
                        .then_inc(gu_hi_ready, 1)

            split_xT(0)
            act.wait_ge(bias_ready, 2)
            for b in range(NB):
                h0 = HEADS * b
                act.wait_ge(xT_ready, KC * (b + 1))
                with act.Fori(0, PAIRS) as p:
                    for u in range(4):
                        unit = 4 * (b * PAIRS + p) + u
                        hh = 2 * p + u % 2
                        src = bank[4 + u][:, :]
                        act.wait_ge(sq_added, unit + 1)
                        act.wait_ge(proj_done, unit + 1)
                        nc.scalar.activation(slots[:, 6 + u % 2, :], src, ACT.Square,
                                             bias=(bq_c, bk_c)[u // 2][:, bass.ds(hh, 1)]).then_inc(squared, 1)
                        if u < 2:
                            nc.scalar.activation(qs[:, hh, :], src, ACT.Identity, bias=bqg[:, bass.ds(hh, 1)],
                                                 scale=gqk[:, bass.ds(hh, 1)]).then_inc(proj_free, 1)
                        else:
                            nc.scalar.activation(ks[:, hh, :], src, ACT.Identity, bias=bk_c[:, bass.ds(hh, 1)])\
                                .then_inc(proj_free, 1)

                def qk_high(hh, i):
                    nc.scalar.activation(qk_hi[:, 1 - i, :], (ks, qs)[i][:, hh, :], ACT.Copy).then_inc(qk_hi_ready, 1)

                def exps(h, e, c):
                    s = TC * e + c
                    act.wait_ge(max_ready, TC * h + c + 1)
                    nc.scalar.activation(slots[:, s, :], slots[:, s, :], ACT.Exp, bias=neg_max[:, s:s + 1],
                                         scale=rq[:, c:c + 1], accum_out=row_sum[:, s:s + 1]).then_inc(exp_done, 1)

                def pT_high(h, j):
                    act.wait_ge(pT_done, TC * h + j + 1)
                    act.wait_ge(pT_used, TC * h + j + 1)
                    nc.scalar.activation(pT_hi[:, j % 2, :], bank[2 + j % 2][:, :], ACT.Copy).then_inc(pT_hi_ready, 1)

                def v_high(pair, half):
                    act.wait_ge(v_done, 2 * pair + half + 1)
                    if half == 0:
                        act.wait_ge(pT_used, TC * 2 * pair + 2)
                    nc.scalar.activation(v_hi[:, 2 * half:2 * half + 2, :],
                                         bank[5 + half][:, :].rearrange("p (c n) -> p c n", c=2),
                                         ACT.Copy).then_inc(v_hi_ready, 1)

                def store_o(h, e, hh):
                    act.wait_ge(pT_used, TC * h + TC + 2)
                    nc.scalar.activation(qs[:, hh, :], bank[O_BANK[e]][:, :], ACT.Identity,
                                         bias=bv_c[:, bass.ds(hh, 1)]).then_inc(o_free, 1)

                act.wait_ge(proj_free, 4 * PAIRS * (b + 1) + 4)
                if b:
                    act.wait_ge(merged, TC * b)
                qk_high(0, 0)
                qk_high(0, 1)
                act.wait_ge(rms_sum, b + 1)
                act.wait_ge(eps_ready, 2)
                nc.scalar.activation(rms[:, :], bank[3][:, 0:2 * TC], ACT.Sqrt, bias=eps[:, 0:1], scale=1.0 / INNER)\
                    .then_inc(rms_step, 1)
                nc.scalar.activation(carrier[:, 0:1], gk_c[:, 0:1], ACT.Exp)
                v_high(PAIRS * b, 0)
                act.wait_ge(rk_spread, b + 1)
                nc.scalar.activation(rk_rows[:, :], bank[2][:, :], ACT.Copy).then_inc(rk_ready, 1)
                for c in range(TC - 1):
                    exps(h0, 0, c)
                act.wait_ge(s_done, TC * (h0 + 1))
                qk_high(1, 0)
                exps(h0, 0, TC - 1)
                qk_high(1, 1)
                v_high(PAIRS * b, 1)

                def head_step(hh, e, last):
                    h = h0 + hh
                    more = not (last and e)
                    pT_high(h, 0)
                    pT_high(h, 1)
                    if more:
                        exps(h + 1, 1 - e, 0)
                    pT_high(h, 2)
                    if more:
                        exps(h + 1, 1 - e, 1)
                    pT_high(h, 3)
                    if more:
                        exps(h + 1, 1 - e, 2)
                    if not last:
                        act.wait_ge(s_done, TC * (h + 2))
                        qk_high(hh + 2, 0)
                    if more:
                        exps(h + 1, 1 - e, 3)
                    if not last:
                        qk_high(hh + 2, 1)
                    store_o(h, e, hh)

                with act.Fori(0, PAIRS - 1) as p:
                    for e in range(2):
                        head_step(2 * p + e, e, False)
                    for half in range(2):
                        v_high(PAIRS * b + p + 1, half)
                for e in range(2):
                    head_step(HEADS - 2 + e, e, True)

                def oT_high(hh):
                    for e in range(2):
                        act.wait_ge(oT_used, (HEADS - 1) * b + hh + e + 1)
                        nc.scalar.activation(qk_hi[:, e, :], qs[:, hh + e, :], ACT.Copy).then_inc(oT_hi_ready, 1)
                act.wait_ge(o_free, HEADS * (b + 1) + 2)
                oT_high(0)
                oT_high(2)
                if b == 0:
                    split_xT(1)
                else:
                    gu_high(0, 0, P)
                    gu_high(0, 1, P)
                    for n in range(TC):
                        x1T_high(n)
                with act.Fori(2, PAIRS) as p:
                    oT_high(2 * p)
                for c in range(TC):
                    ln_root(act, TC * b, c)

            def hidden(n, par, j, b, rows):
                act.wait_ge(gate_done, n + 1)
                act.wait_ge(h_ready, n + 1)
                nc.scalar.activation(act_f[0:rows, par, :], bank[4 + 2 * par][0:rows, :], ACT.Silu).then_inc(silu_done, 1)
                act.wait_ge(h_done, n + 3)
                nc.scalar.activation(hid_hi[0:rows, j, b * S:(b + 1) * S], act_f[0:rows, par, :], ACT.Copy)\
                    .then_inc(h_hi_ready, 1)

            hidden(0, 0, *FIRST[0], P)
            for n in range(TC, 2 * TC):
                x1T_high(n)
            hidden(1, 1, *FIRST[1], P)
            hidden(2, 0, *FIRST[2], P)
            act.wait_ge(x1_out[1], 16 * TC)
            act.wait_ge(up_done, 3)
            gu_high(1, 0, P)
            hidden(3, 1, *FIRST[3], P)
            act.wait_ge(up_done, 4)
            gu_high(1, 1, P)
            with act.Fori(1, GROUPS - 1) as g:
                for jj in range(2):
                    for b in range(NB):
                        hidden(4 * g + 2 * jj + b, b, 2 * g + jj, b, P)
                    act.wait_ge(up_done, 4 * g + 2 * jj + 2)
                    gu_high(g + 1, jj, P)
            g = GROUPS - 1
            for b in range(NB):
                hidden(4 * g + b, b, 2 * g, b, P)
            act.wait_ge(up_done, 4 * g + 2)
            gu_high(GROUPS, 0, REST)
            for b in range(NB):
                hidden(4 * g + 2 + b, b, 2 * g + 1, b, P)

            def wd_high(b, j):
                rows = P if j < FC - 1 else REST
                n = FC * b + j
                act.wait_ge(w_eff, 6 * (j // 2) + 5 + j % 2)
                if n >= 2:
                    free_wd(act, n - 2)
                nc.scalar.activation(wd_hi[0:rows, n % 2, :], wd[0:rows, j, :], ACT.Copy).then_inc(wd_hi_ready, 1)

            wd_high(0, 0)
            wd_high(0, 1)
            for b in range(NB):
                hidden(4 * GROUPS + b, b, 2 * GROUPS, b, REST)
            for b in range(NB):
                for j in range(2 if b == 0 else 0, FC):
                    wd_high(b, j)
                    if b and j == 3:
                        roots_out(act, 0)
            roots_out(act, 1)

        @block.vector
        def _(dve):
            dve.sem_inc(s_free, 2)
            dve.sem_inc(pT_ready, 2)
            dve.sem_inc(h_done, 2)
            def w_high(i, part):
                nc.vector.tensor_copy(flat(w_hi[i], part), flat(w_stage[i], part)).then_inc(w_hi_ready[i], 1)

            def w_low(i, use, part):
                dve.wait_ge(w_hi_ready[i], 2 * use + 1 + part)
                op = nc.vector.tensor_tensor(flat(w_lo[i], part), flat(w_stage[i], part), f(flat(w_hi[i], part)),
                                             ALU.subtract)
                if part:
                    op.then_inc(w_ready[i], 1)

            def split_slab(i, use):
                dve.wait_ge(w_in[i], 16 * (use + 1))
                w_high(i, 0)
                w_high(i, 1)
                w_low(i, use, 0)
                w_low(i, use, 1)

            def split_xT(b):
                for k in range(KC):
                    dve.wait_ge(xT_hi_ready, KC * b + k + 1)
                    nc.vector.tensor_tensor(xT_lo[:, k, :], slots[:, 4 + k, :], f(xT_hi[:, k, :]), ALU.subtract)\
                        .then_inc(xT_ready, 1)

            def split_lora(t, t_f, block_lo, w, count, done):
                nc.vector.tensor_copy(t[0:LK, :, 0:w], t_f[0:LK, :, 0:w]).then_inc(done, 1)
                dve.wait_ge(done, count + 1)
                r = slice(32 * block_lo, 32 * block_lo + RANK)
                nc.vector.tensor_tensor(t[r, :, 0:w], t_f[r, :, 0:w], f(t[r, :, 0:w]), ALU.subtract).then_inc(done, 1)

            def x1T_low(n):
                dve.wait_ge(x1T_hi_ready, n + 1)
                at = slice((n % TC) * P, (n % TC + 1) * P)
                nc.vector.tensor_tensor(x1T_lo[n // TC][:, :, at],
                                        bank[x1T_bank(n)][:, :].rearrange("p (k t) -> p k t", k=KC),
                                        f(x1T_hi[n // TC][:, :, at]), ALU.subtract).then_inc(x1T_ready, 1)

            def fold_gu(g, w, first_bank):
                dve.wait_ge(gu_in, 80 * (g + 1))
                for i in range(2):
                    for half in range(2):
                        dve.wait_ge(fold_done, 6 * g + 2 * i + half + 1)
                        part = gu_stage[i][:, 2 * half:2 * half + 2, 0:w]
                        src = bank[first_bank + 2 * i + half][:, :].rearrange("p (k n) -> p k n", k=2)[:, :, 0:w]
                        nc.vector.tensor_tensor(part, src, part, ALU.add).then_inc(w_eff, 1)

            def fold_down(g, jj, rows):
                dve.wait_ge(fold_done, 6 * g + 5 + jj)
                part = wd[0:rows, bass.ds(2 * g + jj, 1), :].rearrange("p a n -> p (a n)")
                nc.vector.tensor_tensor(part, bank[jj][0:rows, :], part, ALU.add).then_inc(w_eff, 1)

            def gu_low(g, jj, w):
                for i in range(2):
                    dve.wait_ge(gu_hi_ready, 4 * g + 2 * jj + i + 1)
                    nc.vector.tensor_tensor(gu_lo[jj][i][:, :, 0:w], gu_stage[i][:, :, jj * P:jj * P + w],
                                            f(gu_hi[jj][i][:, :, 0:w]), ALU.subtract).then_inc(gu_ready, 1)

            def norm_rows(rows, n0, k0, src_bank, product, residual, loads=None):
                def add(c):
                    dve.wait_ge(product, n0 + c + 1)
                    if residual is not None:
                        dve.wait_ge(residual, n0 + c + 1)
                    else:
                        dve.wait_ge(x1_in[c], 16 * loads)
                    nc.vector.tensor_tensor(rows[:, c, :], bank[src_bank + c][:, :], rows[:, c, :], ALU.add)\
                        .then_inc(ln_sum, 1)

                def invert(c):
                    dve.wait_ge(ln_sqrt, k0 + c + 1)
                    nc.vector.reciprocal(ln_rstd[:, c:c + 1], ln_rstd[:, c:c + 1]).then_inc(ln_inv, 1)

                def apply(c):
                    dve.wait_ge(ln_inv, k0 + c + 1)
                    nc.vector.tensor_scalar(rows[:, c, :], rows[:, c, :], ln_mv[:, c, 0:1], ln_rstd[:, c:c + 1],
                                            ALU.subtract, ALU.mult).then_inc(ln_done, 1)

                add(0)
                for c in range(TC):
                    if c + 1 < TC:
                        add(c + 1)
                    if c:
                        invert(c - 1)
                    dve.wait_ge(ln_sum, k0 + c + 1)
                    nc.vector.bn_stats(ln_stats[:, c, :], rows[:, c, :]).then_inc(ln_stat, 1)
                    if c:
                        apply(c - 1)
                    dve.wait_ge(ln_stat, k0 + c + 1)
                    nc.vector.bn_aggr(ln_mv[:, c, :], ln_stats[:, c, :]).then_inc(ln_mean, 1)
                invert(TC - 1)
                apply(TC - 1)

            dve.wait_ge(const_in, 80)
            nc.vector.tensor_tensor(gqk[:, :], gqk[:, :], gk_c[:, :], ALU.mult).then_inc(bias_ready, 1)
            dve.wait_ge(bias_ready, 1)
            nc.vector.tensor_tensor(bqg[:, :], bq_c[:, :], gqk[:, :], ALU.mult).then_inc(bias_ready, 1)
            split_xT(0)
            for b in range(NB):
                h0 = HEADS * b
                if b:
                    dve.wait_ge(merged, TC * b)
                split_slab(0, use0(b, "project"))
                split_slab(1, use1(b, "project"))
                if b:
                    norm_rows(slots, 0, 0, 0, merged, res_ready)
                with dve.Fori(1, PAIRS) as p:
                    for i in range(2):
                        dve.wait_ge(proj_done, 4 * (PAIRS * b + p) - 2 + 2 * i)
                        split_slab(i, (use0, use1)[i](b, "project") + p)

                dve.wait_ge(proj_done, 4 * PAIRS * (b + 1) - 2)
                split_slab(0, use0(b, "attend"))

                def q_low(h, hh):
                    dve.wait_ge(qk_hi_ready, 2 * h + 2)
                    nc.vector.tensor_tensor(qk_lo[:, 0, :], qs[:, hh, :], f(qk_hi[:, 0, :]), ALU.subtract)\
                        .then_inc(q_ready, 1)

                q_low(h0, 0)
                dve.wait_ge(rms_step, 4 * b + 1)
                nc.vector.reciprocal(rms[:, :], rms[:, :]).then_inc(rms_step, 1)
                dve.wait_ge(rms_step, 4 * b + 2)
                nc.vector.tensor_tensor(slots[:, 5, :].rearrange("p (c t) -> p c t", c=TC),
                                        ident[:, :].rearrange("p (a t) -> p a t", a=1).broadcast_to([P, TC, P]),
                                        rms[:, TC:2 * TC].rearrange("p (c a) -> p c a", a=1).broadcast_to([P, TC, P]),
                                        ALU.mult).then_inc(rms_step, 1)
                nc.vector.tensor_scalar(neg_rq[:, :], rms[:, 0:TC], -(DH ** -0.5), None, ALU.mult)
                nc.vector.tensor_scalar(rq[:, :], rms[:, 0:TC], DH ** -0.5, None, ALU.mult).then_inc(rms_step, 1)

                def scale_scores(h, e, c):
                    s = TC * e + c
                    dve.wait_ge(s_done, TC * h + c + 1)
                    nc.vector.memset(carrier[:, s:s + 1], 0.0)
                    nc.vector.tensor_tensor_reduce(
                        out=slots[:, s, :], in0=bank[c % 2][:, :], in1=rk_rows[:, :], scale=1.0, scalar=FLOAT_MIN,
                        op0=ALU.mult, op1=ALU.max, accum_out=row_max[:, s:s + 1]).then_inc(s_free, 1)

                def normalise(h, e, half):
                    s = TC * e + 2 * half
                    dve.wait_ge(exp_done, TC * h + 2 * half + 2)
                    nc.vector.reciprocal(inv_sum[:, s:s + 2], row_sum[:, s:s + 2]).then_inc(inv_ready, 1)
                    dve.wait_ge(inv_ready, 2 * h + half + 1)
                    for c in range(2):
                        nc.vector.tensor_scalar(slots[:, s + c, :], slots[:, s + c, :], inv_sum[:, s + c:s + c + 1],
                                                None, ALU.mult).then_inc(p_ready, 1)

                def pT_low(h, j):
                    dve.wait_ge(pT_hi_ready, TC * h + j + 1)
                    nc.vector.tensor_tensor(pT_lo[:, j % 2, :], bank[2 + j % 2][:, :], f(pT_hi[:, j % 2, :]),
                                            ALU.subtract).then_inc(pT_ready, 1)

                def v_low(pair, half):
                    dve.wait_ge(v_hi_ready, 2 * pair + half + 1)
                    rows = slice(2 * half, 2 * half + 2)
                    nc.vector.tensor_tensor(v_lo[:, rows, :], bank[5 + half][:, :].rearrange("p (c n) -> p c n", c=2),
                                            f(v_hi[:, rows, :]), ALU.subtract).then_inc(v_ready, 1)

                v_low(PAIRS * b, 0)
                dve.wait_ge(rk_ready, b + 1)
                if b:
                    dve.wait_ge(x1_out[0], 16 * TC)
                for c in range(TC):
                    scale_scores(h0, 0, c)
                for half in range(2):
                    normalise(h0, 0, half)
                q_low(h0 + 1, 1)
                v_low(PAIRS * b, 1)

                def head_step(h, hh, e, last, use=None, pair=None):
                    more = not (last and e)
                    pT_low(h, 0)
                    if more:
                        scale_scores(h + 1, 1 - e, 0)
                    if use is not None:
                        dve.wait_ge(w_in[0], 16 * (use + 1))
                        dve.wait_ge(v_done, 2 * pair + 2)
                        w_high(0, 0)
                    pT_low(h, 1)
                    if more:
                        scale_scores(h + 1, 1 - e, 1)
                    if use is not None:
                        w_high(0, 1)
                    pT_low(h, 2)
                    if more:
                        scale_scores(h + 1, 1 - e, 2)
                    pT_low(h, 3)
                    if more:
                        scale_scores(h + 1, 1 - e, 3)
                        normalise(h + 1, 1 - e, 0)
                        normalise(h + 1, 1 - e, 1)
                    if not last:
                        q_low(h + 2, hh + 2)

                with dve.Fori(0, PAIRS - 1) as p:
                    head_step(h0 + 2 * p, 2 * p, 0, False, use0(b, "attend") + 1 + p, PAIRS * b + p)
                    head_step(h0 + 2 * p + 1, 2 * p + 1, 1, False)
                    for half in range(2):
                        v_low(PAIRS * b + p + 1, half)
                head_step(h0 + HEADS - 2, HEADS - 2, 0, True)
                split_slab(0, use0(b, "merge"))
                head_step(h0 + HEADS - 1, HEADS - 1, 1, True)
                dve.wait_ge(pT_used, TC * HEADS * (b + 1) + 2)
                split_slab(1, use1(b, "merge"))
                if b == 0:
                    split_xT(1)
                else:
                    dve.wait_ge(la_in, 48)
                    split_lora(la, la_f, 2, D, 0, la_ready)
                    dve.wait_ge(gu_in, 80)
                    split_lora(lb, lb_f, 1, W2, 0, lb_ready)
                    fold_gu(0, W2, 4)
                    gu_low(0, 0, P)
                    gu_low(0, 1, P)
                    for n in range(TC):
                        x1T_low(n)
                with dve.Fori(1, PAIRS // 2) as p:
                    for i in range(2):
                        dve.wait_ge(oT_used, (HEADS - 1) * b + 4 * p + 2 * i)
                        split_slab(i, (use0, use1)[i](b, "merge") + p)

            norm_rows(slots, TC, TC, 0, merged, res_ready)

            def hidden(n, par, rows):
                dve.wait_ge(silu_done, n + 1)
                dve.wait_ge(up_done, n + 1)
                nc.vector.tensor_tensor(act_f[0:rows, par, :], bank[5 + 2 * par][0:rows, :], act_f[0:rows, par, :],
                                        ALU.mult).then_inc(h_done, 1)

            def split_lb(g, w):
                dve.wait_ge(gu_in, 80 * (g + 1))
                dve.wait_ge(fold_done, 6 * g)
                split_lora(lb, lb_f, 1, w, 2 * g, lb_ready)

            hidden(0, 0, P)
            for n in range(TC, 2 * TC):
                x1T_low(n)
            hidden(1, 1, P)
            split_lb(1, W2)
            dve.wait_ge(wd_in, 32)
            fold_down(0, 0, P)
            fold_down(0, 1, P)
            hidden(2, 0, P)
            fold_gu(1, W2, 0)
            gu_low(1, 0, P)
            hidden(3, 1, P)
            fold_down(1, 0, P)
            fold_down(1, 1, P)
            gu_low(1, 1, P)
            with dve.Fori(1, GROUPS - 1) as g:
                hidden(4 * g, 0, P)
                split_lb(g + 1, W2)
                hidden(4 * g + 1, 1, P)
                fold_gu(g + 1, W2, 0)
                gu_low(g + 1, 0, P)
                for b in range(NB):
                    hidden(4 * g + 2 + b, b, P)
                fold_down(g + 1, 0, P)
                fold_down(g + 1, 1, P)
                gu_low(g + 1, 1, P)
            g = GROUPS - 1
            hidden(4 * g, 0, P)
            split_lb(GROUPS, REST)
            hidden(4 * g + 1, 1, P)
            fold_gu(GROUPS, REST, 0)
            gu_low(GROUPS, 0, REST)
            for b in range(NB):
                hidden(4 * g + 2 + b, b, P)
            fold_down(GROUPS, 0, REST)

            wd_low(dve, nc.vector, 0, 0)
            wd_low(dve, nc.vector, 0, 1)
            for b in range(NB):
                hidden(4 * GROUPS + b, b, REST)
            for j in range(2, FC):
                wd_low(dve, nc.vector, 0, j)
            norm_rows(x1_rows, 0, 2 * TC, 0, down_done, None, 1)
            norm_rows(x1_rows, TC, 3 * TC, 4, down_done, None, 2)

        @block.tensor
        def _(pe):
            pe.sem_inc(pT_used, 2)
            pe.sem_inc(oT_used, 2)

            def mm3(dst, a, b_, first, last):
                nc.tensor.matmul(dst, a[0], b_[0], start=first, stop=False)
                nc.tensor.matmul(dst, a[0], b_[1], start=False, stop=False)
                return nc.tensor.matmul(dst, a[1], b_[0], start=False, stop=last)

            def transpose_x1(n):
                if n < TC:
                    pe.wait_ge(x1_in[n], 16)
                else:
                    pe.wait_ge(ln_done, n + 1)
                rows = (x1_rows if n < TC else slots)[:, n % TC, :]
                for k in range(KC):
                    last = nc.tensor.transpose(bank[x1T_bank(n)][:, k * P:(k + 1) * P], rows[:, k * P:(k + 1) * P],
                                               ident[:, :])
                last.then_inc(x1T_done, 1)

            def fold_gu(g, w, first_bank):
                pe.wait_ge(lb_ready, 2 * g + 2)
                for i in range(2):
                    for half in range(2):
                        for k in range(2):
                            kc = 2 * half + k
                            last = nc.tensor.matmul(
                                bank[first_bank + 2 * i + half][:, k * W2:k * W2 + w],
                                la[0:LK, i, kc * P:(kc + 1) * P], lb[0:LK, i, 0:w], start=True, stop=True)
                        last.then_inc(fold_done, 1)

            def fold_down(jj, rows):
                nc.tensor.matmul(bank[jj][0:rows, :], lb[0:LK, 2, jj * P:jj * P + rows], la[0:LK, 2, :],
                                 start=True, stop=True).then_inc(fold_done, 1)

            pe.wait_ge(xT_ready, KC)
            for b in range(NB):
                h0 = HEADS * b
                if b:
                    pe.wait_ge(xT_ready, KC * (b + 1))
                    pe.wait_ge(o_free, HEADS * b + 2)
                    pe.wait_ge(v_ready, 2 * PAIRS * b)
                with pe.Fori(0, PAIRS) as p:
                    for u in range(4):
                        unit = 4 * (b * PAIRS + p) + u
                        i, e = u // 2, u % 2
                        if e == 0:
                            pe.wait_ge(w_ready[i], (use0, use1)[i](b, "project") + p + 1)
                        pe.wait_ge(proj_free, unit + 1)
                        for k in range(KC):
                            cols = slice(e * DH, (e + 1) * DH)
                            last = mm3(bank[4 + u][:, :], (w_hi[i][:, k, cols], w_lo[i][:, k, cols]),
                                       (xT_hi[:, k, :], xT_lo[:, k, :]), k == 0, k == KC - 1)
                        last.then_inc(proj_done, 1)

                def values(half, c, use=None):
                    at = (2 * half + c) * P
                    dst = bank[5 + half][:, c * W2:(c + 1) * W2]
                    if use is not None:
                        pe.wait_ge(w_hi_ready[0], 2 * use + 2)
                    for k in range(KC):
                        nc.tensor.matmul(dst, xT_hi[:, k, at:at + P], w_hi[0][:, k, :], start=k == 0, stop=False)
                        nc.tensor.matmul(dst, xT_lo[:, k, at:at + P], w_hi[0][:, k, :], start=False, stop=False)
                    if use is not None:
                        pe.wait_ge(w_ready[0], use + 1)
                    for k in range(KC):
                        last = nc.tensor.matmul(dst, xT_hi[:, k, at:at + P], w_lo[0][:, k, :], start=False,
                                                stop=k == KC - 1)
                    if c:
                        last.then_inc(v_done, 1)

                def scores(h, c):
                    if c == 0:
                        pe.wait_ge(k_ready, h + 1)
                        pe.wait_ge(q_ready, h + 1)
                    pe.wait_ge(s_free, TC * h + c + 1)
                    mm3(bank[c % 2][:, :], [t[:, 0, c * P:(c + 1) * P] for t in (qk_hi, qk_lo)],
                        [t[:, 1, :] for t in (qk_hi, qk_lo)], True, True).then_inc(s_done, 1)

                def transpose_p(h, e, j):
                    if j == 0:
                        pe.wait_ge(p_ready, TC * h + TC)
                    pe.wait_ge(pT_ready, TC * h + j + 1)
                    for c in range(TC):
                        last = nc.tensor.transpose(bank[2 + j % 2][:, c * P:(c + 1) * P],
                                                   slots[:, TC * e + c, j * P:(j + 1) * P], ident[:, :])
                    last.then_inc(pT_done, 1)

                def weighted(h, e, j):
                    if j == 0:
                        pe.wait_ge(o_free, h + 1)
                    pe.wait_ge(pT_ready, TC * h + j + 3)
                    cols = slice(e * DH, (e + 1) * DH)
                    mm3(bank[O_BANK[e]][:, :], (v_hi[:, j, cols], v_lo[:, j, cols]),
                        (pT_hi[:, j % 2, :], pT_lo[:, j % 2, :]), j == 0, j == TC - 1).then_inc(pT_used, 1)

                def sum_squares(i):
                    for c in range(TC):
                        last = nc.tensor.matmul(bank[3][:, TC * i + c:TC * i + c + 1],
                                                slots[:, 4 + i, c * P:(c + 1) * P], ones[:, 0:1], start=True, stop=True)
                    return last

                pe.wait_ge(ones_ready, b + 1)
                if b:
                    pe.wait_ge(ln_sum, TC)
                pe.wait_ge(sq_added, 4 * PAIRS * (b + 1))
                sum_squares(0)
                pe.wait_ge(proj_free, 4 * PAIRS * (b + 1) + 2)
                values(0, 0, use0(b, "attend"))
                pe.wait_ge(sq_added, 4 * PAIRS * (b + 1) + 2)
                sum_squares(1).then_inc(rms_sum, 1)
                values(0, 1)
                scores(h0, 0)
                pe.wait_ge(rms_step, 4 * b + 3)
                nc.tensor.matmul(bank[2][:, :], ones, slots[:, 5, :], start=True, stop=True).then_inc(rk_spread, 1)
                scores(h0, 1)
                pe.wait_ge(proj_free, 4 * PAIRS * (b + 1) + 4)
                values(1, 0)
                scores(h0, 2)
                scores(h0, 3)
                values(1, 1)
                if b == 0:
                    pe.wait_ge(ident_ready, 1)

                def head_step(h, e, last, pair, first_v, second_v):
                    more = not (last and e)

                    def more_scores(c):
                        if more:
                            scores(h + 1, c)
                    transpose_p(h, e, 0)
                    transpose_p(h, e, 1)
                    more_scores(0)
                    more_scores(1)
                    if e == 0:
                        pe.wait_ge(v_ready, 2 * pair + 2)
                    weighted(h, e, 0)
                    transpose_p(h, e, 2)
                    more_scores(2)
                    weighted(h, e, 1)
                    transpose_p(h, e, 3)
                    more_scores(3)
                    weighted(h, e, 2)
                    first_v()
                    weighted(h, e, 3)
                    second_v()

                with pe.Fori(0, PAIRS - 1) as p:
                    for e in range(2):
                        pair = PAIRS * b + p

                        def first_v():
                            pe.wait_ge(v_ready, 2 * pair + e + 1)
                            values(e, 0, use0(b, "attend") + p + 1 if e == 0 else None)
                        head_step(h0 + 2 * p + e, e, False, pair, first_v, lambda: values(e, 1))
                for e in range(2):
                    head_step(h0 + HEADS - 2 + e, e, True, PAIRS * (b + 1) - 1, lambda: None, lambda: None)

                def merge_head(hh, m, first, final):
                    i, e = m // 2, m % 2
                    pe.wait_ge(oT_ready, h0 + hh + 1)
                    rhs = [t[:, 2 * e:2 * e + 2, :].rearrange("p k n -> p (k n)") for t in (w_hi[i], w_lo[i])]
                    for c in range(TC):
                        last = mm3(bank[c][:, :], [t[:, e, c * P:(c + 1) * P] for t in (qk_hi, qk_lo)], rhs, first, final)
                        if final:
                            last.then_inc(merged, 1)
                    if not final:
                        last.then_inc(oT_used, 1)

                def merge_four(p, first, final):
                    for m in range(4):
                        if m % 2 == 0:
                            pe.wait_ge(w_ready[m // 2], (use0, use1)[m // 2](b, "merge") + p + 1)
                        merge_head(4 * p + m, m, first and m == 0, final and m == 3)

                pe.wait_ge(s_free, TC * HEADS * (b + 1) + 2)
                pe.wait_ge(pT_ready, TC * HEADS * (b + 1) + 2)
                merge_four(0, True, False)
                if b == NB - 1:
                    pe.wait_ge(la_ready, 2)
                    pe.wait_ge(o_free, HEADS * NB + 2)
                    pe.wait_ge(v_ready, 2 * PAIRS * NB)
                    fold_gu(0, W2, 4)
                    for n in range(TC):
                        if n < 2:
                            pe.wait_ge(w_eff, n + 1)
                        else:
                            pe.wait_ge(x1T_ready, n - 1)
                        transpose_x1(n)
                with pe.Fori(1, PAIRS // 2 - 1) as p:
                    merge_four(p, False, False)
                merge_four(PAIRS // 2 - 1, False, True)

            def gate_up(n, par, j, jj, b, rows, between=None):
                pe.wait_ge(h_done, n + 1)
                for i in range(2):
                    if i and between:
                        between()
                    pe.wait_ge(gu_ready, 2 * j + i + 1)
                    for k in range(KC):
                        last = mm3(bank[4 + 2 * par + i][0:rows, :],
                                   (gu_hi[jj][i][:, k, 0:rows], gu_lo[jj][i][:, k, 0:rows]),
                                   (x1T_hi[b][:, k, :], x1T_lo[b][:, k, :]), k == 0, k == KC - 1)
                    last.then_inc((gate_done, up_done)[i], 1)

            pe.wait_ge(x1T_ready, TC)
            pe.wait_ge(w_eff, 4)
            def second_x1T():
                for n in range(TC, 2 * TC):
                    transpose_x1(n)
            gate_up(0, 0, 0, 0, 0, P)
            gate_up(1, 1, 1, 1, 0, P, second_x1T)
            for jj in range(2):
                pe.wait_ge(x1T_ready, TC + jj + 1)
                fold_down(jj, P)
            pe.wait_ge(x1T_ready, 2 * TC)
            gate_up(2, 0, 0, 0, 1, P)
            pe.wait_ge(w_eff, 6)
            fold_gu(1, W2, 0)
            gate_up(3, 1, 1, 1, 1, P)
            pe.wait_ge(w_eff, 8)
            fold_down(0, P)
            fold_down(1, P)

            def group(g, next_w, next_down):
                for b in range(NB):
                    gate_up(4 * g + b, b, 2 * g, 0, b, P)
                pe.wait_ge(w_eff, 6 * g + 6)
                fold_gu(g + 1, next_w, 0)
                for b in range(NB):
                    gate_up(4 * g + 2 + b, b, 2 * g + 1, 1, b, P)
                pe.wait_ge(w_eff, 6 * g + 8)
                for jj, rows in enumerate(next_down):
                    fold_down(jj, rows)
            with pe.Fori(1, GROUPS - 1) as g:
                group(g, W2, (P, P))
            group(GROUPS - 1, REST, (REST,))
            for b in range(NB):
                gate_up(4 * GROUPS + b, b, 2 * GROUPS, 0, b, REST)

            pe.wait_ge(w_eff, 6 * GROUPS + 5)
            def down(b, j, c):
                n = FC * b + j
                rows = P if j < FC - 1 else REST
                at = b * S + c * P
                last = mm3(bank[4 * b + c][:, :], (hid_hi[0:rows, j, at:at + P], hid_lo[0:rows, j, at:at + P]),
                           (wd_hi[0:rows, n % 2, :], wd_lo[0:rows, n % 2, :]), j == 0, j == FC - 1)
                if j == FC - 1:
                    last.then_inc(down_done, 1)
                return last

            def down_ready(b, j):
                pe.wait_ge(wd_ready[b], j + 1)
                pe.wait_ge(h_ready, (4 * GROUPS + b if j == FC - 1 else 4 * (FC // 2) - 1 if j > 1 else 3) + 3)

            for b in range(NB):
                if b:
                    pe.wait_ge(h_done, 4 * GROUPS + NB + 2)
                for j in range(FC - 2 if b else FC):
                    down_ready(b, j)
                    for c in range(TC):
                        last = down(b, j, c)
                    if j < FC - 1:
                        last.then_inc(wd_used, 1)
            down_ready(1, FC - 2)
            down_ready(1, FC - 1)
            for c in range(TC):
                down(1, FC - 2, c)
                down(1, FC - 1, c)


def arranged(inputs):
    import numpy as np
    i = {k.replace("L0_", ""): np.asarray(v) for k, v in inputs.items()}
    x = i["attn_hidden_states"].reshape(NB * S, D)

    def by_head(v):
        return v.reshape(HEADS, DH).T
    return {
        "xT": x.T, "x": x, "wq": i["attn_Wq"], "wk": i["attn_Wk"], "wv": i["attn_Wv"], "wo": i["attn_Wo"],
        "bq": by_head(i["attn_bq"]), "bk": by_head(i["attn_bk"]), "bv": by_head(i["attn_bv"]), "bo": i["attn_bo"],
        "gq": by_head(i["attn_gq"]), "gk": by_head(i["attn_gk"]),
        "gate_w": i["ffn_gate_w"].T, "up_w": i["ffn_up_w"].T, "down_w": i["ffn_down_w"].T,
        "lora_a": np.stack([i["ffn_gate_a"], i["ffn_up_a"], i["ffn_down_b"].T], 1),
        "lora_b": np.stack([i["ffn_gate_b"].T, i["ffn_up_b"].T, i["ffn_down_a"]], 1),
    }


def kernel(**inputs):
    import numpy as np
    import concourse.bacc as bacc
    from concourse.bass_utils import run_bass_kernel_spmd

    nc = bacc.Bacc("TRN2", target_bir_lowering=False, num_devices=1)
    arrays, args = {}, []
    for name, a in arranged(inputs).items():
        arrays[name] = np.ascontiguousarray(a)
        args.append(nc.dram_tensor(name, a.shape, mybir.dt.from_np(a.dtype), kind="ExternalInput").ap())
    args.append(nc.dram_tensor("x1_scratch", (NB * S, D), F32, kind="Internal").ap())
    args.append(nc.dram_tensor("out", (NB * S, D), F32, kind="ExternalOutput").ap())
    layer_kernel(nc, *args)
    r = run_bass_kernel_spmd(nc, [arrays], core_ids=[0])
    return r.results[0]["out"].reshape(NB, S, D)
```

```python
import concourse.bass as bass
from concourse import mybir
from contextlib import ExitStack

F32 = mybir.dt.float32
F32R = mybir.dt.float32r
ALU = mybir.AluOpType
ACT = mybir.ActivationFunctionType
AX = mybir.AxisListType

P = 128
NB, S, D = 2, 512, 512
HEADS, DH = 32, 128
INNER = HEADS * DH
FF, RANK = 1376, 16
KC = D // P
TC = S // P
PAIRS = HEADS // 2
W2 = 2 * DH
RMS_EPS, LN_EPS = 1e-6, 1e-5
FLOAT_MIN = -3.4028234e38
GROUPS = FF // W2
REST = FF - GROUPS * W2
FC = GROUPS * 2 + 1
FIRST = ((0, 0), (1, 0), (0, 1), (1, 1))
WARM_UP = 18
LK = 80


def layer_kernel(nc, xT, x, wq, wk, wv, wo, bq, bk, bv, bo, gq, gk,
                 gate_w, up_w, down_w, lora_a, lora_b, x1_dram, out):
    ctx = ExitStack()
    with ctx:
        def sem(name):
            return ctx.enter_context(nc.semaphore(name))

        O_BANK = (4, 7)
        S_BANK = (0, 1, 0, 1)
        FIRST_S = (0, 1, 3, 7)
        XT_ORDER = (2, 3, 0, 1)
        M_BANK = (5, 6, 0, 1)
        FIRST_FOLD = (2, 3, *O_BANK)
        bank = [ctx.enter_context(nc.psum_tensor(f"bank{i}", [P, 512], F32)) for i in range(8)]

        def const(name, shape):
            return ctx.enter_context(nc.sbuf_tensor(name, shape, F32))

        ident = const("ident", [P, P])
        bq_c = const("bq_c", [P, HEADS])
        bk_c = const("bk_c", [P, HEADS])
        bv_c = const("bv_c", [P, HEADS])
        gqk = const("gqk", [P, HEADS])
        gk_c = const("gk_c", [P, HEADS])
        bqg = const("bqg", [P, HEADS])
        eps = const("eps", [P, 2])
        rms = const("rms", [P, 2 * TC])
        rq = const("rq", [P, TC])
        neg_rq = const("neg_rq", [P, TC])
        row_max = const("row_max", [P, 8])
        neg_max = const("neg_max", [P, 8])
        carrier = const("carrier", [P, 8])
        row_sum = const("row_sum", [P, 8])
        inv_sum = const("inv_sum", [P, 8])
        ln_stats = const("ln_stats", [P, TC, 6])
        ln_mv = const("ln_mv", [P, TC, 2])
        ln_rstd = const("ln_rstd", [P, TC])

        with ExitStack() as region:
            def sa(name, shape, dt=F32):
                return region.enter_context(nc.sbuf_tensor(name, shape, dt))
            ks = sa("ks", [P, HEADS, S])
            qs = sa("qs", [P, HEADS, S])
            w_stage = [sa(f"w_stage{i}", [P, KC, W2]) for i in range(2)]
            slots = sa("slots", [P, 8, S])
            xT_hi = sa("xT_hi", [P, KC, S], F32R)
            xT_lo = sa("xT_lo", [P, KC, S], F32R)
            w_hi = [sa(f"w_hi{i}", [P, KC, W2], F32R) for i in range(2)]
            w_lo = [sa(f"w_lo{i}", [P, KC, W2], F32R) for i in range(2)]
            qk_hi = sa("qk_hi", [P, 2, S], F32R)
            qk_lo = sa("qk_lo", [P, 2, S], F32R)
            pT_hi = sa("pT_hi", [P, 2, S], F32R)
            pT_lo = sa("pT_lo", [P, 2, S], F32R)
            rk_rows = sa("rk_rows", [P, S])
            bo_rows = sa("bo_rows", [P, D])
        v_hi, v_lo = w_hi[1], w_lo[1]

        def oT_buffers(m, early):
            if early:
                return xT_hi[:, m, :], xT_lo[:, m, :]
            if m < 2:
                return pT_hi[:, m, :], pT_lo[:, m, :]
            return [t[:, 2 * m - 4:2 * m - 2, :].rearrange("p k n -> p (k n)") for t in (v_hi, v_lo)]
        ones = bo_rows[:, 0:P]

        with ExitStack() as region:
            def sf(name, shape, dt=F32):
                return region.enter_context(nc.sbuf_tensor(name, shape, dt))
            x1_rows = sf("x1_rows", [P, 4, D])
            lb_f = sf("lb_f", [P, 3, W2])
            la = sf("la", [P, 3, D], F32R)
            lb = sf("lb", [P, 3, W2], F32R)
            gu_stage = [sf(f"gu_stage{i}", [P, KC, W2]) for i in range(2)]
            gu_hi = [[sf(f"gu_hi{j}{i}", [P, KC, P], F32R) for i in range(2)] for j in range(2)]
            gu_lo = [[sf(f"gu_lo{j}{i}", [P, KC, P], F32R) for i in range(2)] for j in range(2)]
            x1T_hi = [sf("x1T_hi0", [P, KC, S], F32R)]
            x1T_lo = [sf("x1T_lo0", [P, KC, S], F32R)]
            x1T_hi.append(sf("x1T_hi1", [P, KC, S], F32R))
            x1T_lo.append(sf("x1T_lo1", [P, KC, S], F32R))
            wd = sf("wd", [P, FC, D])
            wd_hi = sf("wd_hi", [P, 2, D], F32R)
            wd_lo = sf("wd_lo", [P, 2, D], F32R)
            hid_hi = sf("hid_hi", [P, FC, NB * S], F32R)
            hid_lo = sf("hid_lo", [P, FC, NB * S], F32R)
            act_f = sf("act_f", [P, 2, S])
        la_f = x1_rows[:, 0:3, :]

        def f(ap):
            return ap.bitcast(F32)

        const_in = sem("const_in")
        ident_zero = sem("ident_zero")
        ident_ready = sem("ident_ready")
        ones_ready = sem("ones_ready")
        eps_ready = sem("eps_ready")
        bias_ready = sem("bias_ready")
        x_in = sem("x_in")
        xT_hi_ready = sem("xT_hi_ready")
        xT_first = sem("xT_first")
        xT_ready = sem("xT_ready")
        w_in = [sem(f"w_in{i}") for i in range(2)]
        w_hi_ready = [sem(f"w_hi_ready{i}") for i in range(2)]
        w_ready = [sem(f"w_ready{i}") for i in range(2)]
        acc_zero = sem("acc_zero")
        proj_done = sem("proj_done")
        squared = sem("squared")
        proj_free = sem("proj_free")
        sq_added = sem("sq_added")
        rms_sum = sem("rms_sum")
        rms_step = sem("rms_step")
        rk_spread = sem("rk_spread")
        rk_ready = sem("rk_ready")
        qk_hi_ready = sem("qk_hi_ready")
        k_ready = sem("k_ready")
        q_ready = sem("q_ready")
        s_done = sem("s_done")
        s_free = sem("s_free")
        max_ready = sem("max_ready")
        exp_done = sem("exp_done")
        inv_ready = sem("inv_ready")
        p_ready = sem("p_ready")
        pT_done = sem("pT_done")
        pT_hi_ready = sem("pT_hi_ready")
        pT_ready = sem("pT_ready")
        pT_used = sem("pT_used")
        o_free = sem("o_free")
        v_done = sem("v_done")
        v_hi_ready = sem("v_hi_ready")
        v_ready = sem("v_ready")
        oT_hi_ready = sem("oT_hi_ready")
        oT_first = sem("oT_first")
        oT_ready = sem("oT_ready")
        oT_used = sem("oT_used")
        res_in = sem("res_in")
        res_ready = sem("res_ready")
        merged = sem("merged")
        ln_sum = sem("ln_sum")
        ln_stat = sem("ln_stat")
        ln_mean = sem("ln_mean")
        ln_sqrt = sem("ln_sqrt")
        ln_inv = sem("ln_inv")
        ln_done = sem("ln_done")
        x1_out = [sem(f"x1_out{i}") for i in range(NB)]
        la_in = sem("la_in")
        lora_zero = sem("lora_zero")
        la_ready = sem("la_ready")
        gu_in = sem("gu_in")
        lb_ready = sem("lb_ready")
        fold_done = sem("fold_done")
        w_eff = sem("w_eff")
        gu_hi_ready = sem("gu_hi_ready")
        gu_ready = sem("gu_ready")
        wd_in = sem("wd_in")
        x1_in = [sem(f"x1_in{i}") for i in range(4)]
        x1T_done = sem("x1T_done")
        x1T_hi_ready = sem("x1T_hi_ready")
        x1T_ready = sem("x1T_ready")
        gate_done = sem("gate_done")
        up_done = sem("up_done")
        silu_done = sem("silu_done")
        h_done = sem("h_done")
        h_hi_ready = sem("h_hi_ready")
        h_ready = sem("h_ready")
        wd_hi_ready = sem("wd_hi_ready")
        wd_ready = [sem(f"wd_ready{b}") for b in range(NB)]
        wd_used = sem("wd_used")
        down_done = sem("down_done")
        out_done = [sem(f"out_done{i}") for i in range(4)]

        USES = (2 * PAIRS + PAIRS // 2, PAIRS + PAIRS // 2)

        def use0(b, phase):
            return b * USES[0] + {"project": 0, "attend": PAIRS, "merge": 2 * PAIRS}[phase]

        def use1(b, phase):
            return b * USES[1] + {"project": 0, "merge": PAIRS}[phase]

        def wait_xT(eng, b):
            if b == 0:
                eng.wait_ge(xT_first, 2)
            eng.wait_ge(xT_ready, KC * (b + 1) - 2)

        def free_wd(eng, n):
            if n % FC == FC - 1:
                eng.wait_ge(down_done, TC * (n // FC + 1))
            else:
                eng.wait_ge(wd_used, (FC - 1) * (n // FC) + n % FC + 1)

        def ln_root(act, k0, c):
            act.wait_ge(ln_mean, k0 + c + 1)
            nc.scalar.activation(ln_rstd[:, c:c + 1], ln_mv[:, c, 1:2], ACT.Sqrt, bias=eps[:, 1:2]).then_inc(ln_sqrt, 1)

        def wd_buffer(n):
            i = n % 4
            if i < 2:
                return wd_hi[:, i, :], wd_lo[:, i, :]
            return [t[1][i - 2][:, :, :].rearrange("p k n -> p (k n)") for t in (gu_hi, gu_lo)]

        def wd_low(eng, ops, b, j):
            rows = P if j < FC - 1 else REST
            n = FC * b + j
            eng.wait_ge(wd_hi_ready, n + 1)
            hi, lo = wd_buffer(n)
            ops.tensor_tensor(lo[0:rows, :], wd[0:rows, j, :], f(hi[0:rows, :]), ALU.subtract).then_inc(wd_ready[b], 1)

        def x1T_bank(n):
            return O_BANK[n % 2] if n < TC else (2, 3, 0, 1)[n - TC]

        def flat(t, part):
            half = KC * W2 // 2
            return t[:, :, :].rearrange("p k n -> p (k n)")[:, part * half:(part + 1) * half]

        block = ctx.enter_context(nc.Block())

        @block.sync
        def _(sp):
            wq_v, wk_v, wv_v, gate_v, up_v = (w.rearrange("(k p) n -> p k n", p=P)
                                              for w in (wq, wk, wv, gate_w, up_w))
            wo_v = wo.rearrange("(h p) n -> p h n", p=P)
            x1_v = x1_dram.rearrange("(c p) d -> p c d", p=P)

            def load_w(i, use, src):
                sp.wait_ge(w_ready[i], use)
                sp.dma_start(w_stage[i][:, :, :], src).then_inc(w_in[i], 16)

            def load_qk(b, p):
                load_w(0, use0(b, "project") + p, wq_v[:, :, bass.ds(p * W2, W2)])
                load_w(1, use1(b, "project") + p, wk_v[:, :, bass.ds(p * W2, W2)])

            def load_wo(b, p):
                for i in range(2):
                    sp.wait_ge(w_ready[i], (use0, use1)[i](b, "merge") + p)
                    sp.dma_start(w_stage[i][:, :, :].rearrange("p k n -> p (k n)").rearrange("p (h n) -> p h n", h=2),
                                 wo_v[:, bass.ds(4 * p + 2 * i, 2), :]).then_inc(w_in[i], 16)

            def load_xT(b):
                sp.dma_start(slots[:, 4:8, :], xT[:, b * S:(b + 1) * S].rearrange("(k p) t -> p k t", p=P))\
                    .then_inc(x_in, 16)

            def load_gu(g, w):
                sp.dma_start(gu_stage[0][:, :, 0:w], gate_v[:, :, bass.ds(g * W2, w)]).then_inc(gu_in, 16)
                sp.dma_start(gu_stage[1][:, :, 0:w], up_v[:, :, bass.ds(g * W2, w)]).then_inc(gu_in, 16)
                for r in range(3):
                    sp.dma_start(lb_f[32 * r:32 * r + RANK, :, 0:w], lora_b[:, :, bass.ds(g * W2, w)])\
                        .then_inc(gu_in, 16)

            def load_x1(n):
                sp.dma_start(x1_rows[:, n % 4, :], x1_v[:, n, :]).then_inc(x1_in[n % 4], 16)

            def store_out(b, c):
                sp.wait_ge(ln_done, TC * (NB + b) + c + 1)
                sp.dma_start(out[(TC * b + c) * P:(TC * b + c + 1) * P, :], x1_rows[:, c, :]).then_inc(out_done[c], 16)

            load_xT(0)
            sp.dma_start(w_stage[0][:, :, :], wq_v[:, :, 0:W2]).then_inc(w_in[0], 16)
            sp.dma_start(w_stage[1][:, :, :], wk_v[:, :, 0:W2]).then_inc(w_in[1], 16)
            for dst, src in ((bq_c, bq), (bk_c, bk), (bv_c, bv), (gqk, gq), (gk_c, gk)):
                sp.dma_start(dst[:, :], src).then_inc(const_in, 16)
            for b in range(NB):
                if b:
                    load_qk(b, 0)
                with sp.Fori(1, PAIRS) as p:
                    load_qk(b, p)
                with sp.Fori(0, PAIRS) as p:
                    load_w(0, use0(b, "attend") + p, wv_v[:, :, bass.ds(p * W2, W2)])
                load_wo(b, 0)
                load_wo(b, 1)
                sp.wait_ge(pT_done, TC * HEADS * (b + 1))
                if b == 0:
                    load_xT(1)
                sp.dma_start(slots[:, 0:TC, :], x[b * S:(b + 1) * S, :].rearrange("(c p) d -> p c d", p=P))\
                    .then_inc(res_in, 16)
                sp.dma_start(bo_rows[:, :], bo.partition_broadcast(P)).then_inc(res_in, 16)
                if b == NB - 1:
                    sp.wait_ge(lora_zero, 2)
                    for r in range(3):
                        sp.dma_start(la_f[32 * r:32 * r + RANK, :, :], lora_a).then_inc(la_in, 16)
                    load_gu(0, W2)
                    sp.wait_ge(la_ready, 2)
                    sp.wait_ge(x1_out[0], 16 * TC)
                    for n in range(TC):
                        load_x1(n)
                with sp.Fori(2, PAIRS // 2) as p:
                    load_wo(b, p)

            sp.wait_ge(gu_ready, 4)
            sp.wait_ge(lb_ready, 2)
            load_gu(1, W2)
            sp.wait_ge(merged, TC * NB)
            sp.dma_start(wd[:, 0:2 * GROUPS, :], down_w[0:GROUPS * W2, :].rearrange("(j p) n -> p j n", p=P))\
                .then_inc(wd_in, 16)
            sp.dma_start(wd[0:REST, 2 * GROUPS, :], down_w[GROUPS * W2:FF, :]).then_inc(wd_in, 16)
            with sp.Fori(2, GROUPS) as g:
                sp.wait_ge(gu_ready, 4 * g)
                load_gu(g, W2)
            sp.wait_ge(gu_ready, 4 * GROUPS)
            sp.wait_ge(lb_ready, 2 * GROUPS)
            load_gu(GROUPS, REST)
            sp.wait_ge(x1_out[1], 16 * TC)
            for c in range(TC):
                store_out(0, c)
            for n in range(TC, 2 * TC):
                sp.wait_ge(out_done[n % 4], 16)
                load_x1(n)
            for c in range(TC):
                store_out(1, c)
            for i in range(4):
                sp.wait_ge(out_done[i], 32)

        @block.gpsimd
        def _(pool):
            pool.sem_inc(sq_added, 2)
            pool.sem_inc(h_ready, 2)
            pool.memset(ident[:, :], 0.0).then_inc(ident_zero, 1)
            pool.memset(ones, 1.0).then_inc(ones_ready, 1)
            pool.memset(eps[:, 0:1], RMS_EPS).then_inc(eps_ready, 1)
            pool.memset(eps[:, 1:2], LN_EPS).then_inc(eps_ready, 1)
            pool.wait_ge(ident_zero, 1)
            pool.affine_select(out=ident[:, :], in_=ident[:, :], compare_op=ALU.not_equal, fill=1.0,
                               base=0, pattern=[[-1, P]], channel_multiplier=1).then_inc(ident_ready, 1)
            for i in range(2):
                k = XT_ORDER[i]
                pool.wait_ge(xT_hi_ready, i + 1)
                nc.gpsimd.tensor_tensor(xT_lo[:, k, :], slots[:, 4 + k, :], f(xT_hi[:, k, :]), ALU.subtract)\
                    .then_inc(xT_first, 1)
            for b in range(NB):
                h0 = HEADS * b
                wait_xT(pool, b)
                pool.memset(slots[:, 4:6, :], 0.0).then_inc(acc_zero, 1)
                if b:
                    pool.memset(ones, 1.0).then_inc(ones_ready, 1)
                pool.wait_ge(acc_zero, b + 1)
                with pool.Fori(0, PAIRS) as p:
                    for u in range(4):
                        unit = 4 * (b * PAIRS + p) + u
                        pool.wait_ge(squared, unit + 1)
                        pool.wait_ge(sq_added, unit + 2)
                        acc = slots[:, 4 + u // 2, :]
                        nc.gpsimd.tensor_tensor(acc, acc, slots[:, 6 + u % 2, :], ALU.add).then_inc(sq_added, 1)

                def k_low(h, hh):
                    pool.wait_ge(qk_hi_ready, 2 * h + 1)
                    nc.gpsimd.tensor_tensor(qk_lo[:, 1, :], ks[:, hh, :], f(qk_hi[:, 1, :]), ALU.subtract)\
                        .then_inc(k_ready, 1)

                def neg_maxima(h, e, c):
                    s = TC * e + c
                    pool.wait_ge(s_free, TC * h + c + 3)
                    nc.gpsimd.tensor_tensor(neg_max[:, s:s + 1], row_max[:, s:s + 1], neg_rq[:, c:c + 1],
                                            ALU.mult).then_inc(max_ready, 1)

                def slab_low(use, part):
                    pool.wait_ge(w_hi_ready[0], 2 * use + part + 1)
                    op = nc.gpsimd.tensor_tensor(flat(w_lo[0], part), flat(w_stage[0], part), f(flat(w_hi[0], part)),
                                                 ALU.subtract)
                    if part:
                        op.then_inc(w_ready[0], 1)

                k_low(h0, 0)
                pool.wait_ge(rms_step, 4 * b + 4)
                for c in range(TC):
                    neg_maxima(h0, 0, c)
                k_low(h0 + 1, 1)
                with pool.Fori(0, PAIRS - 1) as p:
                    for e in range(2):
                        hh = 2 * p + e
                        for c in range(TC):
                            neg_maxima(h0 + hh + 1, 1 - e, c)
                            if e == 0 and c < 2:
                                slab_low(use0(b, "attend") + p + 1, c)
                        k_low(h0 + hh + 2, hh + 2)

                def oT_low(hh, m, early):
                    pool.wait_ge(oT_hi_ready, h0 + hh + 1)
                    hi, lo = oT_buffers(m, early)
                    nc.gpsimd.tensor_tensor(lo, qs[:, hh, :], f(hi), ALU.subtract).then_inc(oT_ready, 1)

                for c in range(TC):
                    neg_maxima(h0 + HEADS - 1, 1, c)
                    if c < 2:
                        slab_low(use0(b, "merge"), c)
                    if c == 1:
                        oT_low(1, 1, True)
                if b == NB - 1:
                    pool.wait_ge(s_done, TC * HEADS * NB)
                    pool.memset(la_f, 0.0).then_inc(lora_zero, 1)
                    pool.memset(lb_f[:, :, :], 0.0).then_inc(lora_zero, 1)
                oT_low(2, 2, True)
                oT_low(3, 3, True)
                for m in range(4):
                    oT_low(4 + m, m, False)
                pool.wait_ge(res_in, 32 * (b + 1))
                for c in range(TC):
                    nc.gpsimd.tensor_tensor(slots[:, c, :], slots[:, c, :], bo_rows[:, :], ALU.add)\
                        .then_inc(res_ready, 1)
                with pool.Fori(2, PAIRS // 2) as p:
                    for m in range(4):
                        oT_low(4 * p + m, m, False)
                for c in range(TC):
                    pool.wait_ge(ln_done, TC * b + c + 1)
                    pool.dma_start(x1_dram[(TC * b + c) * P:(TC * b + c + 1) * P, :], slots[:, c, :])\
                        .then_inc(x1_out[b], 16)

            def hid_low(n, par, j, b, rows):
                pool.wait_ge(h_hi_ready, n + 1)
                nc.gpsimd.tensor_tensor(hid_lo[0:rows, j, b * S:(b + 1) * S], act_f[0:rows, par, :],
                                        f(hid_hi[0:rows, j, b * S:(b + 1) * S]), ALU.subtract).then_inc(h_ready, 1)
            for n, (j, b) in enumerate(FIRST):
                hid_low(n, n % 2, j, b, P)
            with pool.Fori(1, GROUPS) as g:
                for jj in range(2):
                    for b in range(NB):
                        hid_low(4 * g + 2 * jj + b, b, 2 * g + jj, b, P)
            for b in range(NB):
                hid_low(4 * GROUPS + b, b, 2 * GROUPS, b, REST)
            for j in range(FC):
                wd_low(pool, nc.gpsimd, 1, j)

        @block.scalar
        def _(act):
            act.sem_inc(proj_free, 4)
            act.sem_inc(o_free, 2)

            def split_xT(b):
                act.wait_ge(x_in, 16 * (b + 1))
                for k in XT_ORDER:
                    nc.scalar.activation(xT_hi[:, k, :], slots[:, 4 + k, :], ACT.Copy).then_inc(xT_hi_ready, 1)

            def x1T_high(n):
                act.wait_ge(x1T_done, n + 1)
                nc.scalar.activation(x1T_hi[n // TC][:, :, (n % TC) * P:(n % TC + 1) * P],
                                     bank[x1T_bank(n)][:, :].rearrange("p (k t) -> p k t", k=KC), ACT.Copy)\
                    .then_inc(x1T_hi_ready, 1)

            def gu_high(g, jj, w):
                act.wait_ge(w_eff, 6 * g + 4)
                for i in range(2):
                    nc.scalar.activation(gu_hi[jj][i][:, :, 0:w], gu_stage[i][:, :, jj * P:jj * P + w], ACT.Copy)\
                        .then_inc(gu_hi_ready, 1)

            split_xT(0)
            act.wait_ge(eps_ready, 2)
            nc.scalar.activation(carrier[:, 0:1], eps[:, 0:1], ACT.Sqrt)
            act.wait_ge(bias_ready, 2)
            for b in range(NB):
                h0 = HEADS * b
                wait_xT(act, b)
                with act.Fori(0, PAIRS) as p:
                    for u in range(4):
                        unit = 4 * (b * PAIRS + p) + u
                        hh = 2 * p + u % 2
                        src = bank[4 + u][:, :]
                        act.wait_ge(sq_added, unit + 1)
                        act.wait_ge(proj_done, unit + 1)
                        nc.scalar.activation(slots[:, 6 + u % 2, :], src, ACT.Square,
                                             bias=(bq_c, bk_c)[u // 2][:, bass.ds(hh, 1)]).then_inc(squared, 1)
                        if u < 2:
                            nc.scalar.activation(qs[:, hh, :], src, ACT.Identity, bias=bqg[:, bass.ds(hh, 1)],
                                                 scale=gqk[:, bass.ds(hh, 1)]).then_inc(proj_free, 1)
                        else:
                            nc.scalar.activation(ks[:, hh, :], src, ACT.Identity, bias=bk_c[:, bass.ds(hh, 1)])\
                                .then_inc(proj_free, 1)

                def qk_high(hh, i):
                    nc.scalar.activation(qk_hi[:, 1 - i, :], (ks, qs)[i][:, hh, :], ACT.Copy).then_inc(qk_hi_ready, 1)

                def exps(h, e, c):
                    s = TC * e + c
                    act.wait_ge(max_ready, TC * h + c + 1)
                    nc.scalar.activation(slots[:, s, :], slots[:, s, :], ACT.Exp, bias=neg_max[:, s:s + 1],
                                         scale=rq[:, c:c + 1], accum_out=row_sum[:, s:s + 1]).then_inc(exp_done, 1)

                def pT_high(h, j):
                    act.wait_ge(pT_done, TC * h + j + 1)
                    act.wait_ge(pT_used, TC * h + j + 1)
                    nc.scalar.activation(pT_hi[:, j % 2, :], bank[2 + j % 2][:, :], ACT.Copy).then_inc(pT_hi_ready, 1)

                def v_high(pair, half):
                    act.wait_ge(v_done, 2 * pair + half + 1)
                    nc.scalar.activation(v_hi[:, 2 * half:2 * half + 2, :],
                                         bank[5 + half][:, :].rearrange("p (c n) -> p c n", c=2),
                                         ACT.Copy).then_inc(v_hi_ready, 1)

                def store_o(h, e, hh):
                    act.wait_ge(pT_used, TC * h + TC + 2)
                    nc.scalar.activation(qs[:, hh, :], bank[O_BANK[e]][:, :], ACT.Identity,
                                         bias=bv_c[:, bass.ds(hh, 1)]).then_inc(o_free, 1)

                act.wait_ge(proj_free, 4 * PAIRS * (b + 1) + 4)
                if b:
                    act.wait_ge(merged, TC * b)
                qk_high(0, 0)
                qk_high(0, 1)
                act.wait_ge(rms_sum, b + 1)
                act.wait_ge(eps_ready, 2)
                nc.scalar.activation(rms[:, :], bank[3][:, 0:2 * TC], ACT.Sqrt, bias=eps[:, 0:1], scale=1.0 / INNER)\
                    .then_inc(rms_step, 1)
                nc.scalar.activation(carrier[:, 0:1], gk_c[:, 0:1], ACT.Exp)
                v_high(PAIRS * b, 0)
                act.wait_ge(rk_spread, b + 1)
                nc.scalar.activation(rk_rows[:, :], bank[2][:, :], ACT.Copy).then_inc(rk_ready, 1)
                for c in range(TC):
                    exps(h0, 0, c)
                for i in range(2):
                    qk_high(1, i)
                v_high(PAIRS * b, 1)

                def oT_high(hh, m, early=False):
                    nc.scalar.activation(oT_buffers(m, early)[0], qs[:, hh, :], ACT.Copy).then_inc(oT_hi_ready, 1)

                def head_step(hh, e, last, next_pair=None):
                    h = h0 + hh
                    more = not (last and e)
                    pT_high(h, 0)
                    pT_high(h, 1)
                    if last and not e:
                        act.wait_ge(v_done, 2 * PAIRS * (b + 1))
                        oT_high(0, 0, True)
                        oT_high(1, 1, True)
                    if more:
                        exps(h + 1, 1 - e, 0)
                    pT_high(h, 2)
                    if more:
                        exps(h + 1, 1 - e, 1)
                    pT_high(h, 3)
                    if next_pair is not None:
                        act.wait_ge(pT_used, TC * h + 4)
                        v_high(next_pair, 0)
                    if more:
                        exps(h + 1, 1 - e, 2)
                    if not last:
                        act.wait_ge(s_done, TC * (h + 2))
                        qk_high(hh + 2, 0)
                    if more:
                        exps(h + 1, 1 - e, 3)
                    if not last:
                        qk_high(hh + 2, 1)
                    store_o(h, e, hh)
                    if last and not e:
                        oT_high(2, 2, True)
                        oT_high(3, 3, True)

                with act.Fori(0, PAIRS - 1) as p:
                    head_step(2 * p, 0, False)
                    head_step(2 * p + 1, 1, False, PAIRS * b + p + 1)
                    v_high(PAIRS * b + p + 1, 1)
                for e in range(2):
                    head_step(HEADS - 2 + e, e, True)

                def oT_high_four(p):
                    for m in range(4):
                        act.wait_ge(oT_used, (HEADS - 1) * b + 4 * p + m - 3)
                        oT_high(4 * p + m, m)
                act.wait_ge(o_free, HEADS * (b + 1) + 2)
                act.wait_ge(pT_used, TC * HEADS * (b + 1) + 2)
                oT_high_four(1)
                if b == 0:
                    act.wait_ge(oT_used, 4)
                    split_xT(1)
                    with act.Fori(2, PAIRS // 2) as p:
                        oT_high_four(p)
                else:
                    oT_high_four(2)
                    gu_high(0, 0, P)
                    gu_high(0, 1, P)
                    for n in range(0, TC, 2):
                        oT_high_four(3 + n // 2)
                        x1T_high(n)
                        x1T_high(n + 1)
                    with act.Fori(5, PAIRS // 2) as p:
                        oT_high_four(p)
                for c in range(TC):
                    ln_root(act, TC * b, c)

            def hidden(n, par, j, b, rows):
                act.wait_ge(gate_done, n + 1)
                act.wait_ge(h_ready, n + 1)
                nc.scalar.activation(act_f[0:rows, par, :], bank[4 + 2 * par][0:rows, :], ACT.Silu).then_inc(silu_done, 1)
                act.wait_ge(h_done, n + 3)
                nc.scalar.activation(hid_hi[0:rows, j, b * S:(b + 1) * S], act_f[0:rows, par, :], ACT.Copy)\
                    .then_inc(h_hi_ready, 1)

            hidden(0, 0, *FIRST[0], P)
            for n in range(TC, 2 * TC):
                x1T_high(n)
            hidden(1, 1, *FIRST[1], P)
            hidden(2, 0, *FIRST[2], P)
            act.wait_ge(x1_out[1], 16 * TC)
            act.wait_ge(up_done, 3)
            gu_high(1, 0, P)
            hidden(3, 1, *FIRST[3], P)
            act.wait_ge(up_done, 4)
            gu_high(1, 1, P)
            with act.Fori(1, GROUPS - 1) as g:
                for jj in range(2):
                    for b in range(NB):
                        hidden(4 * g + 2 * jj + b, b, 2 * g + jj, b, P)
                    act.wait_ge(up_done, 4 * g + 2 * jj + 2)
                    gu_high(g + 1, jj, P)
            g = GROUPS - 1
            for b in range(NB):
                hidden(4 * g + b, b, 2 * g, b, P)
            act.wait_ge(up_done, 4 * g + 2)
            gu_high(GROUPS, 0, REST)
            for b in range(NB):
                hidden(4 * g + 2 + b, b, 2 * g + 1, b, P)

            def wd_high(b, j):
                rows = P if j < FC - 1 else REST
                n = FC * b + j
                act.wait_ge(w_eff, 6 * (j // 2) + 5 + j % 2)
                if n >= 4:
                    free_wd(act, n - 4)
                elif n >= 2:
                    act.wait_ge(up_done, 4 * GROUPS)
                nc.scalar.activation(wd_buffer(n)[0][0:rows, :], wd[0:rows, j, :], ACT.Copy).then_inc(wd_hi_ready, 1)

            wd_high(0, 0)
            wd_high(0, 1)
            for b in range(NB):
                hidden(4 * GROUPS + b, b, 2 * GROUPS, b, REST)
            for b in range(NB):
                for j in range(2 if b == 0 else 0, FC):
                    wd_high(b, j)
                    if b and 4 <= j < 4 + TC:
                        ln_root(act, TC * NB, j - 4)
            for c in range(TC):
                ln_root(act, TC * (NB + 1), c)

        @block.vector
        def _(dve):
            dve.sem_inc(s_free, 2)
            dve.sem_inc(pT_ready, 2)
            dve.sem_inc(h_done, 2)
            def w_high(i, part, hi=None):
                dst = flat(w_hi[i], part) if hi is None else hi[:, part, :]
                nc.vector.tensor_copy(dst, flat(w_stage[i], part)).then_inc(w_hi_ready[i], 1)

            def w_low(i, use, part, hi=None, lo=None):
                dve.wait_ge(w_hi_ready[i], 2 * use + 1 + part)
                if hi is None:
                    dst, high = flat(w_lo[i], part), flat(w_hi[i], part)
                else:
                    dst, high = lo[:, part, :], hi[:, part, :]
                op = nc.vector.tensor_tensor(dst, flat(w_stage[i], part), f(high), ALU.subtract)
                if part:
                    op.then_inc(w_ready[i], 1)

            def split_slab(i, use, hi=None, lo=None):
                dve.wait_ge(w_in[i], 16 * (use + 1))
                w_high(i, 0, hi)
                w_high(i, 1, hi)
                w_low(i, use, 0, hi, lo)
                w_low(i, use, 1, hi, lo)

            def split_xT(b):
                for i, k in enumerate(XT_ORDER):
                    if b or i >= 2:
                        dve.wait_ge(xT_hi_ready, KC * b + i + 1)
                        nc.vector.tensor_tensor(xT_lo[:, k, :], slots[:, 4 + k, :], f(xT_hi[:, k, :]), ALU.subtract)\
                            .then_inc(xT_ready, 1)

            def split_lora(t, t_f, block_lo, w, count, done):
                nc.vector.tensor_copy(t[0:LK, :, 0:w], t_f[0:LK, :, 0:w]).then_inc(done, 1)
                dve.wait_ge(done, count + 1)
                r = slice(32 * block_lo, 32 * block_lo + RANK)
                nc.vector.tensor_tensor(t[r, :, 0:w], t_f[r, :, 0:w], f(t[r, :, 0:w]), ALU.subtract).then_inc(done, 1)

            def x1T_low(n):
                dve.wait_ge(x1T_hi_ready, n + 1)
                at = slice((n % TC) * P, (n % TC + 1) * P)
                nc.vector.tensor_tensor(x1T_lo[n // TC][:, :, at],
                                        bank[x1T_bank(n)][:, :].rearrange("p (k t) -> p k t", k=KC),
                                        f(x1T_hi[n // TC][:, :, at]), ALU.subtract).then_inc(x1T_ready, 1)

            def fold_gu(g, w, banks=range(4)):
                dve.wait_ge(gu_in, 80 * (g + 1))
                for i in range(2):
                    for half in range(2):
                        dve.wait_ge(fold_done, 6 * g + 2 * i + half + 1)
                        part = gu_stage[i][:, 2 * half:2 * half + 2, 0:w]
                        src = bank[banks[2 * i + half]][:, :].rearrange("p (k n) -> p k n", k=2)[:, :, 0:w]
                        nc.vector.tensor_tensor(part, src, part, ALU.add).then_inc(w_eff, 1)

            def fold_down(g, jj, rows):
                dve.wait_ge(fold_done, 6 * g + 5 + jj)
                part = wd[0:rows, bass.ds(2 * g + jj, 1), :].rearrange("p a n -> p (a n)")
                nc.vector.tensor_tensor(part, bank[jj][0:rows, :], part, ALU.add).then_inc(w_eff, 1)

            def gu_low(g, jj, w):
                for i in range(2):
                    dve.wait_ge(gu_hi_ready, 4 * g + 2 * jj + i + 1)
                    nc.vector.tensor_tensor(gu_lo[jj][i][:, :, 0:w], gu_stage[i][:, :, jj * P:jj * P + w],
                                            f(gu_hi[jj][i][:, :, 0:w]), ALU.subtract).then_inc(gu_ready, 1)

            def norm_rows(rows, n0, k0, banks, product, residual, loads=None, between=None):
                def add(c):
                    dve.wait_ge(product, n0 + c + 1)
                    if residual is not None:
                        dve.wait_ge(residual, n0 + c + 1)
                    else:
                        dve.wait_ge(x1_in[c], 16 * loads)
                    nc.vector.tensor_tensor(rows[:, c, :], bank[banks[c]][:, :], rows[:, c, :], ALU.add)\
                        .then_inc(ln_sum, 1)

                def invert(c):
                    dve.wait_ge(ln_sqrt, k0 + c + 1)
                    nc.vector.reciprocal(ln_rstd[:, c:c + 1], ln_rstd[:, c:c + 1]).then_inc(ln_inv, 1)

                def apply(c):
                    dve.wait_ge(ln_inv, k0 + c + 1)
                    nc.vector.tensor_scalar(rows[:, c, :], rows[:, c, :], ln_mv[:, c, 0:1], ln_rstd[:, c:c + 1],
                                            ALU.subtract, ALU.mult).then_inc(ln_done, 1)

                for c in range(TC):
                    add(c)
                    if c:
                        invert(c - 1)
                    dve.wait_ge(ln_sum, k0 + c + 1)
                    nc.vector.bn_stats(ln_stats[:, c, :], rows[:, c, :]).then_inc(ln_stat, 1)
                    dve.wait_ge(ln_stat, k0 + c + 1)
                    nc.vector.bn_aggr(ln_mv[:, c, :], ln_stats[:, c, :]).then_inc(ln_mean, 1)
                    if c:
                        apply(c - 1)
                    if c == 1 and between:
                        between()
                invert(TC - 1)
                apply(TC - 1)

            for b in range(NB):
                h0 = HEADS * b
                if b:
                    dve.wait_ge(oT_used, (HEADS - 1) * b - 1)
                split_slab(0, use0(b, "project"))
                if b == 0:
                    split_xT(0)
                if b:
                    def second_slab():
                        dve.wait_ge(merged, TC * b)
                        split_slab(1, use1(b, "project"))
                    norm_rows(slots, 0, 0, M_BANK, merged, res_ready, between=second_slab)
                else:
                    dve.wait_ge(const_in, 80)
                    nc.vector.tensor_tensor(gqk[:, :], gqk[:, :], gk_c[:, :], ALU.mult).then_inc(bias_ready, 1)
                    dve.wait_ge(bias_ready, 1)
                    nc.vector.tensor_tensor(bqg[:, :], bq_c[:, :], gqk[:, :], ALU.mult).then_inc(bias_ready, 1)
                    split_slab(1, use1(b, "project"))
                with dve.Fori(1, PAIRS) as p:
                    for i in range(2):
                        dve.wait_ge(proj_done, 4 * (PAIRS * b + p) - 2 + 2 * i)
                        split_slab(i, (use0, use1)[i](b, "project") + p)

                dve.wait_ge(proj_done, 4 * PAIRS * (b + 1) - 2)
                split_slab(0, use0(b, "attend"))

                def q_low(h, hh):
                    dve.wait_ge(qk_hi_ready, 2 * h + 2)
                    nc.vector.tensor_tensor(qk_lo[:, 0, :], qs[:, hh, :], f(qk_hi[:, 0, :]), ALU.subtract)\
                        .then_inc(q_ready, 1)

                q_low(h0, 0)
                dve.wait_ge(rms_step, 4 * b + 1)
                nc.vector.reciprocal(rms[:, :], rms[:, :]).then_inc(rms_step, 1)
                dve.wait_ge(rms_step, 4 * b + 2)
                nc.vector.tensor_tensor(slots[:, 5, :].rearrange("p (c t) -> p c t", c=TC),
                                        ident[:, :].rearrange("p (a t) -> p a t", a=1).broadcast_to([P, TC, P]),
                                        rms[:, TC:2 * TC].rearrange("p (c a) -> p c a", a=1).broadcast_to([P, TC, P]),
                                        ALU.mult).then_inc(rms_step, 1)
                nc.vector.tensor_scalar(neg_rq[:, :], rms[:, 0:TC], -(DH ** -0.5), None, ALU.mult)
                nc.vector.tensor_scalar(rq[:, :], rms[:, 0:TC], DH ** -0.5, None, ALU.mult).then_inc(rms_step, 1)

                def scale_scores(h, e, c, s_banks=S_BANK):
                    s = TC * e + c
                    dve.wait_ge(s_done, TC * h + c + 1)
                    nc.vector.memset(carrier[:, s:s + 1], 0.0)
                    nc.vector.tensor_tensor_reduce(
                        out=slots[:, s, :], in0=bank[s_banks[c]][:, :], in1=rk_rows[:, :], scale=1.0, scalar=FLOAT_MIN,
                        op0=ALU.mult, op1=ALU.max, accum_out=row_max[:, s:s + 1]).then_inc(s_free, 1)

                def normalise(h, e, half, next_pair=None):
                    s = TC * e + 2 * half
                    dve.wait_ge(exp_done, TC * h + 2 * half + 2)
                    nc.vector.reciprocal(inv_sum[:, s:s + 2], row_sum[:, s:s + 2]).then_inc(inv_ready, 1)
                    if next_pair is not None:
                        v_low(next_pair, 0)
                    dve.wait_ge(inv_ready, 2 * h + half + 1)
                    for c in range(2):
                        nc.vector.tensor_scalar(slots[:, s + c, :], slots[:, s + c, :], inv_sum[:, s + c:s + c + 1],
                                                None, ALU.mult).then_inc(p_ready, 1)

                def pT_low(h, j):
                    dve.wait_ge(pT_hi_ready, TC * h + j + 1)
                    nc.vector.tensor_tensor(pT_lo[:, j % 2, :], bank[2 + j % 2][:, :], f(pT_hi[:, j % 2, :]),
                                            ALU.subtract).then_inc(pT_ready, 1)

                def v_low(pair, half):
                    dve.wait_ge(v_hi_ready, 2 * pair + half + 1)
                    rows = slice(2 * half, 2 * half + 2)
                    nc.vector.tensor_tensor(v_lo[:, rows, :], bank[5 + half][:, :].rearrange("p (c n) -> p c n", c=2),
                                            f(v_hi[:, rows, :]), ALU.subtract).then_inc(v_ready, 1)

                v_low(PAIRS * b, 0)
                dve.wait_ge(rk_ready, b + 1)
                if b:
                    dve.wait_ge(x1_out[0], 16 * TC)
                for c in range(TC):
                    scale_scores(h0, 0, c, FIRST_S)
                for half in range(2):
                    normalise(h0, 0, half)
                q_low(h0 + 1, 1)
                v_low(PAIRS * b, 1)

                def head_step(h, hh, e, last, use=None, pair=None, next_pair=None):
                    pT_low(h, 0)
                    scale_scores(h + 1, 1 - e, 0)
                    if use is not None:
                        dve.wait_ge(w_in[0], 16 * (use + 1))
                        dve.wait_ge(v_done, 2 * pair + 2)
                        w_high(0, 0)
                    pT_low(h, 1)
                    scale_scores(h + 1, 1 - e, 1)
                    if use is not None:
                        w_high(0, 1)
                    if last:
                        dve.wait_ge(oT_hi_ready, h0 + 1)
                        hi, lo = oT_buffers(0, True)
                        nc.vector.tensor_tensor(lo, qs[:, 0, :], f(hi), ALU.subtract).then_inc(oT_first, 1)
                    pT_low(h, 2)
                    scale_scores(h + 1, 1 - e, 2)
                    pT_low(h, 3)
                    scale_scores(h + 1, 1 - e, 3)
                    normalise(h + 1, 1 - e, 0, next_pair)
                    normalise(h + 1, 1 - e, 1)
                    if not last:
                        q_low(h + 2, hh + 2)

                with dve.Fori(0, PAIRS - 1) as p:
                    head_step(h0 + 2 * p, 2 * p, 0, False, use0(b, "attend") + 1 + p, PAIRS * b + p)
                    head_step(h0 + 2 * p + 1, 2 * p + 1, 1, False, next_pair=PAIRS * b + p + 1)
                    v_low(PAIRS * b + p + 1, 1)
                head_step(h0 + HEADS - 2, HEADS - 2, 0, True, use0(b, "merge"), PAIRS * (b + 1) - 1)
                dve.wait_ge(s_done, TC * HEADS * (b + 1))
                use = use1(b, "merge")
                dve.wait_ge(w_in[1], 16 * (use + 1))
                for part in range(2):
                    w_high(1, part, qk_hi)
                for j in range(TC):
                    pT_low(h0 + HEADS - 1, j)
                    if j < 2:
                        w_low(1, use, j, qk_hi, qk_lo)

                def split_wo(p, slabs=(0, 1)):
                    for i in slabs:
                        dve.wait_ge(oT_used, (HEADS - 1) * b + 4 * p - 2 + 2 * i)
                        split_slab(i, (use0, use1)[i](b, "merge") + p, *((qk_hi, qk_lo) if i else ()))
                if b == 0:
                    split_wo(1)
                    split_xT(1)
                    with dve.Fori(2, PAIRS // 2) as p:
                        split_wo(p)
                else:
                    split_wo(1, (0,))
                    dve.wait_ge(la_in, 48)
                    split_lora(la, la_f, 2, D, 0, la_ready)
                    split_wo(1, (1,))
                    dve.wait_ge(gu_in, 80)
                    split_lora(lb, lb_f, 1, W2, 0, lb_ready)
                    split_wo(2, (0,))
                    fold_gu(0, W2, FIRST_FOLD)
                    split_wo(2, (1,))
                    gu_low(0, 0, P)
                    gu_low(0, 1, P)
                    for n in range(0, TC, 2):
                        split_wo(3 + n // 2)
                        x1T_low(n)
                        x1T_low(n + 1)
                    with dve.Fori(5, PAIRS // 2) as p:
                        split_wo(p)

            norm_rows(slots, TC, TC, M_BANK, merged, res_ready)

            def hidden(n, par, rows):
                dve.wait_ge(silu_done, n + 1)
                dve.wait_ge(up_done, n + 1)
                nc.vector.tensor_tensor(act_f[0:rows, par, :], bank[5 + 2 * par][0:rows, :], act_f[0:rows, par, :],
                                        ALU.mult).then_inc(h_done, 1)

            def split_lb(g, w):
                dve.wait_ge(gu_in, 80 * (g + 1))
                dve.wait_ge(fold_done, 6 * g)
                split_lora(lb, lb_f, 1, w, 2 * g, lb_ready)

            hidden(0, 0, P)
            for n in range(TC, 2 * TC):
                x1T_low(n)
            hidden(1, 1, P)
            split_lb(1, W2)
            dve.wait_ge(wd_in, 32)
            fold_down(0, 0, P)
            fold_down(0, 1, P)
            hidden(2, 0, P)
            fold_gu(1, W2)
            gu_low(1, 0, P)
            hidden(3, 1, P)
            fold_down(1, 0, P)
            fold_down(1, 1, P)
            gu_low(1, 1, P)
            with dve.Fori(1, GROUPS - 1) as g:
                hidden(4 * g, 0, P)
                split_lb(g + 1, W2)
                hidden(4 * g + 1, 1, P)
                fold_gu(g + 1, W2)
                gu_low(g + 1, 0, P)
                for b in range(NB):
                    hidden(4 * g + 2 + b, b, P)
                fold_down(g + 1, 0, P)
                fold_down(g + 1, 1, P)
                gu_low(g + 1, 1, P)
            g = GROUPS - 1
            hidden(4 * g, 0, P)
            split_lb(GROUPS, REST)
            hidden(4 * g + 1, 1, P)
            fold_gu(GROUPS, REST)
            gu_low(GROUPS, 0, REST)
            for b in range(NB):
                hidden(4 * g + 2 + b, b, P)
            fold_down(GROUPS, 0, REST)

            wd_low(dve, nc.vector, 0, 0)
            wd_low(dve, nc.vector, 0, 1)
            for b in range(NB):
                hidden(4 * GROUPS + b, b, REST)
            for j in range(2, FC):
                wd_low(dve, nc.vector, 0, j)
            norm_rows(x1_rows, 0, 2 * TC, range(4), down_done, None, 1)
            norm_rows(x1_rows, TC, 3 * TC, range(4, 8), down_done, None, 2)

        @block.tensor
        def _(pe):
            pe.sem_inc(pT_used, 2)

            def mm3(dst, a, b_, first, last):
                nc.tensor.matmul(dst, a[0], b_[0], start=first, stop=False)
                nc.tensor.matmul(dst, a[0], b_[1], start=False, stop=False)
                return nc.tensor.matmul(dst, a[1], b_[0], start=False, stop=last)

            def transpose_x1(n):
                if n < TC:
                    pe.wait_ge(x1_in[n], 16)
                else:
                    pe.wait_ge(ln_done, n + 1)
                rows = (x1_rows if n < TC else slots)[:, n % TC, :]
                for k in range(KC):
                    last = nc.tensor.transpose(bank[x1T_bank(n)][:, k * P:(k + 1) * P], rows[:, k * P:(k + 1) * P],
                                               ident[:, :])
                last.then_inc(x1T_done, 1)

            def fold_gu(g, w, banks=range(4)):
                pe.wait_ge(lb_ready, 2 * g + 2)
                for i in range(2):
                    for half in range(2):
                        for k in range(2):
                            kc = 2 * half + k
                            last = nc.tensor.matmul(
                                bank[banks[2 * i + half]][:, k * W2:k * W2 + w],
                                la[0:LK, i, kc * P:(kc + 1) * P], lb[0:LK, i, 0:w], start=True, stop=True)
                        last.then_inc(fold_done, 1)

            def fold_down(jj, rows):
                nc.tensor.matmul(bank[jj][0:rows, :], lb[0:LK, 2, jj * P:jj * P + rows], la[0:LK, 2, :],
                                 start=True, stop=True).then_inc(fold_done, 1)

            for b in range(NB):
                h0 = HEADS * b
                if b == 0:
                    pe.wait_ge(ident_ready, 1)
                    for _ in range(WARM_UP):
                        nc.tensor.matmul(bank[0][:, 0:P], ident[:, :], ident[:, :], start=True, stop=True)
                    first = bank[4][:, :]
                    pe.wait_ge(xT_hi_ready, KC)
                    pe.wait_ge(w_hi_ready[0], 2)
                    pe.wait_ge(proj_free, 1)
                    for k in range(KC):
                        nc.tensor.matmul(first, w_hi[0][:, k, 0:DH], xT_hi[:, k, :], start=k == 0, stop=False)
                    pe.wait_ge(w_ready[0], 1)
                    for k in range(KC):
                        nc.tensor.matmul(first, w_lo[0][:, k, 0:DH], xT_hi[:, k, :], start=False, stop=False)
                    wait_xT(pe, 0)
                    for k in range(KC):
                        last = nc.tensor.matmul(first, w_hi[0][:, k, 0:DH], xT_lo[:, k, :], start=False,
                                                stop=k == KC - 1)
                    last.then_inc(proj_done, 1)
                else:
                    wait_xT(pe, b)
                    pe.wait_ge(o_free, HEADS * b + 2)
                def project(p, u):
                    unit = 4 * (b * PAIRS + p) + u
                    i, e = u // 2, u % 2
                    if e == 0:
                        pe.wait_ge(w_ready[i], (use0, use1)[i](b, "project") + p + 1)
                    pe.wait_ge(proj_free, unit + 1)
                    for k in range(KC):
                        cols = slice(e * DH, (e + 1) * DH)
                        last = mm3(bank[4 + u][:, :], (w_hi[i][:, k, cols], w_lo[i][:, k, cols]),
                                   (xT_hi[:, k, :], xT_lo[:, k, :]), k == 0, k == KC - 1)
                    last.then_inc(proj_done, 1)

                if b:
                    project(0, 0)
                    pe.wait_ge(ln_sum, 2)
                for u in range(1, 4):
                    project(0, u)
                with pe.Fori(1, PAIRS) as p:
                    for u in range(4):
                        project(p, u)

                def values(half, c, use=None):
                    at = (2 * half + c) * P
                    dst = bank[5 + half][:, c * W2:(c + 1) * W2]
                    if use is not None:
                        pe.wait_ge(w_hi_ready[0], 2 * use + 2)
                    for k in range(KC):
                        nc.tensor.matmul(dst, xT_hi[:, k, at:at + P], w_hi[0][:, k, :], start=k == 0, stop=False)
                        nc.tensor.matmul(dst, xT_lo[:, k, at:at + P], w_hi[0][:, k, :], start=False, stop=False)
                    if use is not None:
                        pe.wait_ge(w_ready[0], use + 1)
                    for k in range(KC):
                        last = nc.tensor.matmul(dst, xT_hi[:, k, at:at + P], w_lo[0][:, k, :], start=False,
                                                stop=k == KC - 1)
                    if c:
                        last.then_inc(v_done, 1)

                def scores(h, c, s_banks=S_BANK):
                    if c == 0:
                        pe.wait_ge(k_ready, h + 1)
                        pe.wait_ge(q_ready, h + 1)
                    if s_banks == S_BANK:
                        pe.wait_ge(s_free, TC * h + c + 1)
                    mm3(bank[s_banks[c]][:, :], [t[:, 0, c * P:(c + 1) * P] for t in (qk_hi, qk_lo)],
                        [t[:, 1, :] for t in (qk_hi, qk_lo)], True, True).then_inc(s_done, 1)

                def transpose_p(h, e, j):
                    pe.wait_ge(pT_ready, TC * h + j + 1)
                    for c in range(TC):
                        if j == 0 and c % 2 == 0:
                            pe.wait_ge(p_ready, TC * h + c + 2)
                        last = nc.tensor.transpose(bank[2 + j % 2][:, c * P:(c + 1) * P],
                                                   slots[:, TC * e + c, j * P:(j + 1) * P], ident[:, :])
                    last.then_inc(pT_done, 1)

                def weighted(h, e, j):
                    if j == 0:
                        pe.wait_ge(o_free, h + 1)
                    pe.wait_ge(pT_ready, TC * h + j + 3)
                    cols = slice(e * DH, (e + 1) * DH)
                    mm3(bank[O_BANK[e]][:, :], (v_hi[:, j, cols], v_lo[:, j, cols]),
                        (pT_hi[:, j % 2, :], pT_lo[:, j % 2, :]), j == 0, j == TC - 1).then_inc(pT_used, 1)

                def sum_squares(i):
                    for c in range(TC):
                        last = nc.tensor.matmul(bank[3][:, TC * i + c:TC * i + c + 1],
                                                slots[:, 4 + i, c * P:(c + 1) * P], ones[:, 0:1], start=True, stop=True)
                    return last

                pe.wait_ge(ones_ready, b + 1)
                if b:
                    pe.wait_ge(ln_sum, TC)
                pe.wait_ge(sq_added, 4 * PAIRS * (b + 1))
                sum_squares(0)
                pe.wait_ge(proj_free, 4 * PAIRS * (b + 1) + 2)
                values(0, 0, use0(b, "attend"))
                pe.wait_ge(sq_added, 4 * PAIRS * (b + 1) + 2)
                sum_squares(1).then_inc(rms_sum, 1)
                values(0, 1)
                pe.wait_ge(rms_step, 4 * b + 3)
                nc.tensor.matmul(bank[2][:, :], ones, slots[:, 5, :], start=True, stop=True).then_inc(rk_spread, 1)
                pe.wait_ge(rms_step, 4 * b + 1)
                pe.wait_ge(proj_free, 4 * PAIRS * (b + 1) + 4)
                for c in range(TC):
                    scores(h0, c, FIRST_S)
                values(1, 0)
                values(1, 1)
                def head_step(h, e, last, pair, fillers):
                    more = not (last and e)

                    def more_scores(c):
                        if more:
                            scores(h + 1, c)
                    transpose_p(h, e, 0)
                    transpose_p(h, e, 1)
                    fillers[0]()
                    more_scores(0)
                    more_scores(1)
                    if e == 0:
                        pe.wait_ge(v_ready, 2 * pair + 2)
                    weighted(h, e, 0)
                    transpose_p(h, e, 2)
                    fillers[1]()
                    more_scores(2)
                    weighted(h, e, 1)
                    transpose_p(h, e, 3)
                    more_scores(3)
                    fillers[2]()
                    weighted(h, e, 2)
                    fillers[3]()
                    weighted(h, e, 3)
                    fillers[4]()

                def nothing():
                    pass

                with pe.Fori(0, PAIRS - 1) as p:
                    for e in range(2):
                        pair = PAIRS * b + p

                        def first_v():
                            pe.wait_ge(v_ready, 2 * pair + e + 1)
                            values(e, 0, use0(b, "attend") + p + 1 if e == 0 else None)
                        head_step(h0 + 2 * p + e, e, False, pair,
                                  (nothing, nothing, nothing, first_v, lambda: values(e, 1)))

                def merge_part(hh, m, c, early=False, first=False, final=False):
                    i, e = m // 2, m % 2
                    if c == 0:
                        if early and m == 0:
                            pe.wait_ge(oT_first, b + 1)
                        else:
                            pe.wait_ge(oT_ready, (HEADS - 1) * b + hh)
                    if i:
                        wo_parts = [t[:, e, :] for t in (qk_hi, qk_lo)]
                    else:
                        wo_parts = [t[:, 2 * e:2 * e + 2, :].rearrange("p k n -> p (k n)") for t in (w_hi[0], w_lo[0])]
                    last = mm3(bank[M_BANK[c]][:, :], [t[:, c * P:(c + 1) * P] for t in oT_buffers(m, early)],
                               wo_parts, first, final)
                    if final:
                        last.then_inc(merged, 1)
                    elif c == TC - 1:
                        last.then_inc(oT_used, 1)

                def first_two(c, heads=(0, 1)):
                    for hh in heads:
                        merge_part(hh, hh, c, early=True, first=hh == 0)

                def first_chunk():
                    pe.wait_ge(w_ready[0], use0(b, "merge") + 1)
                    first_two(0)

                head_step(h0 + HEADS - 2, 0, True, PAIRS * (b + 1) - 1,
                          (nothing, nothing, nothing, first_chunk, lambda: first_two(1)))

                def third_chunk():
                    pe.wait_ge(s_free, TC * HEADS * (b + 1) + 2)
                    first_two(2)

                def head_two():
                    pe.wait_ge(w_ready[1], use1(b, "merge") + 1)
                    for c in range(2):
                        merge_part(2, 2, c, early=True)

                head_step(h0 + HEADS - 1, 1, True, PAIRS * (b + 1) - 1,
                          (third_chunk, lambda: first_two(3, (0,)), lambda: first_two(3, (1,)), head_two, nothing))
                for c in range(2, TC):
                    merge_part(2, 2, c, early=True)
                for c in range(TC):
                    merge_part(3, 3, c, early=True)

                def merge_four(p, final=False):
                    for m in range(4):
                        if m % 2 == 0:
                            pe.wait_ge(w_ready[m // 2], (use0, use1)[m // 2](b, "merge") + p + 1)
                        for c in range(TC):
                            merge_part(4 * p + m, m, c, final=final and m == 3)

                merge_four(1)
                if b == 0:
                    with pe.Fori(2, PAIRS // 2 - 1) as p:
                        merge_four(p)
                else:
                    pe.wait_ge(la_ready, 2)
                    pe.wait_ge(pT_ready, TC * HEADS * NB + 2)
                    pe.wait_ge(o_free, HEADS * NB + 2)
                    fold_gu(0, W2, FIRST_FOLD)
                    merge_four(2)
                    for n in range(TC):
                        if n < 2:
                            pe.wait_ge(w_eff, n + 3)
                        else:
                            pe.wait_ge(x1T_ready, n - 1)
                        transpose_x1(n)
                        if n == 1:
                            merge_four(3)
                    with pe.Fori(4, PAIRS // 2 - 1) as p:
                        merge_four(p)
                merge_four(PAIRS // 2 - 1, True)

            def gate_up(n, par, j, jj, b, rows, between=None):
                pe.wait_ge(h_done, n + 1)
                for i in range(2):
                    if i and between:
                        between()
                    pe.wait_ge(gu_ready, 2 * j + i + 1)
                    for k in range(KC):
                        last = mm3(bank[4 + 2 * par + i][0:rows, :],
                                   (gu_hi[jj][i][:, k, 0:rows], gu_lo[jj][i][:, k, 0:rows]),
                                   (x1T_hi[b][:, k, :], x1T_lo[b][:, k, :]), k == 0, k == KC - 1)
                    last.then_inc((gate_done, up_done)[i], 1)

            pe.wait_ge(x1T_ready, TC)
            def second_x1T():
                for n in range(TC, 2 * TC):
                    transpose_x1(n)
            gate_up(0, 0, 0, 0, 0, P, lambda: pe.wait_ge(ln_sum, TC + 2))
            gate_up(1, 1, 1, 1, 0, P, second_x1T)
            pe.wait_ge(x1T_ready, 2 * TC)
            for jj in range(2):
                fold_down(jj, P)
            gate_up(2, 0, 0, 0, 1, P)
            pe.wait_ge(w_eff, 6)
            fold_gu(1, W2)
            gate_up(3, 1, 1, 1, 1, P)
            pe.wait_ge(w_eff, 8)
            fold_down(0, P)
            fold_down(1, P)

            def group(g, next_w, next_down):
                for b in range(NB):
                    gate_up(4 * g + b, b, 2 * g, 0, b, P)
                pe.wait_ge(w_eff, 6 * g + 6)
                fold_gu(g + 1, next_w)
                for b in range(NB):
                    gate_up(4 * g + 2 + b, b, 2 * g + 1, 1, b, P)
                pe.wait_ge(w_eff, 6 * g + 8)
                for jj, rows in enumerate(next_down):
                    fold_down(jj, rows)
            with pe.Fori(1, GROUPS - 1) as g:
                group(g, W2, (P, P))
            group(GROUPS - 1, REST, (REST,))
            for b in range(NB):
                gate_up(4 * GROUPS + b, b, 2 * GROUPS, 0, b, REST)

            pe.wait_ge(w_eff, 6 * GROUPS + 5)
            def down(b, j, c):
                n = FC * b + j
                rows = P if j < FC - 1 else REST
                at = b * S + c * P
                last = mm3(bank[4 * b + c][:, :], (hid_hi[0:rows, j, at:at + P], hid_lo[0:rows, j, at:at + P]),
                           [t[0:rows, :] for t in wd_buffer(n)], j == 0, j == FC - 1)
                if j == FC - 1:
                    last.then_inc(down_done, 1)
                return last

            def down_ready(b, j):
                pe.wait_ge(wd_ready[b], j + 1)
                pe.wait_ge(h_ready, (4 * GROUPS + b if j == FC - 1 else 4 * (FC // 2) - 1 if j > 1 else 3) + 3)

            for b in range(NB):
                if b:
                    pe.wait_ge(h_done, 4 * GROUPS + NB + 2)
                for j in range(FC - 3 if b else FC):
                    down_ready(b, j)
                    for c in range(TC):
                        last = down(b, j, c)
                    if j < FC - 1:
                        last.then_inc(wd_used, 1)
            for c in range(TC):
                for j in range(FC - 3, FC):
                    if c == 0:
                        down_ready(1, j)
                    down(1, j, c)


def arranged(inputs):
    import numpy as np
    i = {k.replace("L0_", ""): np.asarray(v) for k, v in inputs.items()}
    x = i["attn_hidden_states"].reshape(NB * S, D)

    def by_head(v):
        return v.reshape(HEADS, DH).T
    return {
        "xT": x.T, "x": x, "wq": i["attn_Wq"], "wk": i["attn_Wk"], "wv": i["attn_Wv"], "wo": i["attn_Wo"],
        "bq": by_head(i["attn_bq"]), "bk": by_head(i["attn_bk"]), "bv": by_head(i["attn_bv"]), "bo": i["attn_bo"],
        "gq": by_head(i["attn_gq"]), "gk": by_head(i["attn_gk"]),
        "gate_w": i["ffn_gate_w"].T, "up_w": i["ffn_up_w"].T, "down_w": i["ffn_down_w"].T,
        "lora_a": np.stack([i["ffn_gate_a"], i["ffn_up_a"], i["ffn_down_b"].T], 1),
        "lora_b": np.stack([i["ffn_gate_b"].T, i["ffn_up_b"].T, i["ffn_down_a"]], 1),
    }


def kernel(**inputs):
    import numpy as np
    import concourse.bacc as bacc
    from concourse.bass_utils import run_bass_kernel_spmd

    nc = bacc.Bacc("TRN2", target_bir_lowering=False, num_devices=1)
    arrays, args = {}, []
    for name, a in arranged(inputs).items():
        arrays[name] = np.ascontiguousarray(a)
        args.append(nc.dram_tensor(name, a.shape, mybir.dt.from_np(a.dtype), kind="ExternalInput").ap())
    args.append(nc.dram_tensor("x1_scratch", (NB * S, D), F32, kind="Internal").ap())
    args.append(nc.dram_tensor("out", (NB * S, D), F32, kind="ExternalOutput").ap())
    layer_kernel(nc, *args)
    r = run_bass_kernel_spmd(nc, [arrays], core_ids=[0])
    return r.results[0]["out"].reshape(NB, S, D)
```
